# Optimizing a Trainium2 kernel written in Bass

```python
import numpy as np
import jax
import jax.numpy as jnp

def _softmax(x, axis=-1):
    return jax.nn.softmax(x, axis=axis)

def _gelu(x):
    return jax.nn.gelu(x, approximate=True)

def _silu(x):
    return jax.nn.silu(x)

def _sigmoid(x):
    return jax.nn.sigmoid(x)

def _layernorm(x, axis=-1, eps=1e-05):
    m = jnp.mean(x, axis=axis, keepdims=True)
    v = jnp.var(x, axis=axis, keepdims=True)
    return (x - m) / jnp.sqrt(v + eps)

def _scatter_add(tgt, idx, src, axis=0):
    return tgt.at[idx].add(src)

def _segment_sum(src, seg, n):
    return jax.ops.segment_sum(src, seg, n)
kernel_name = 'mk_gnn_preln_d2_gnn_r8_a7d9f8'

def setup_inputs(seed: int=0):
    np.random.seed(seed)
    _w = jnp.asarray

    def _rec_inputs():
        import jax
        import jax.numpy as jnp
        _gk = jax.random.key(seed)
        x = -0.0005121 + 1.001 * jax.random.normal(jax.random.fold_in(_gk, 1), (12500, 32), jnp.float32)
        src = jax.random.randint(jax.random.fold_in(_gk, 2), (400000,), 0, 12500, jnp.int32)
        dst = jnp.minimum((12500 * jax.random.uniform(jax.random.fold_in(_gk, 3), (400000,)) ** 2.0).astype(jnp.int32), 99999)
        _o = jnp.argsort(dst, stable=True)
        src = src[_o]
        dst = dst[_o]
        edge_attr_16 = -3.57403e-05 + 0.999761 * jax.random.normal(jax.random.fold_in(_gk, 11), (400000, 16), jnp.float32)
        edge_weight = jax.random.uniform(jax.random.fold_in(_gk, 14), (400000,), jnp.float32, 0.0, 0.999999)
        return (x, src, dst, edge_attr_16, edge_weight)
    x, src, dst, edge_attr_16, edge_weight = _rec_inputs()

    def _L0_gnn_setup():
        import jax, jax.numpy as jnp
        import numpy as np
        N_ATOMS = 12500
        N_EDGES = 37500
        ATOM_DIM = 32
        BOND_DIM = 16
        STEPS = 4

        def _gru_cell(x, h, W_ih, W_hh, b_ih, b_hh):
            gi = x @ W_ih.T + b_ih
            gh = h @ W_hh.T + b_hh
            i_r, i_z, i_n = jnp.split(gi, 3, axis=-1)
            h_r, h_z, h_n = jnp.split(gh, 3, axis=-1)
            r = jax.nn.sigmoid(i_r + h_r)
            z = jax.nn.sigmoid(i_z + h_z)
            n = jnp.tanh(i_n + r * h_n)
            return (1.0 - z) * n + z * h
        key = jax.random.key(seed)
        ks = jax.random.split(key, 8)
        atom_features = jax.random.normal(ks[0], (N_ATOMS, ATOM_DIM), dtype=jnp.float32)
        bond_features = jax.random.normal(ks[1], (N_EDGES, BOND_DIM), dtype=jnp.float32)
        pair_indices = jax.random.randint(ks[2], (N_EDGES, 2), 0, N_ATOMS, dtype=jnp.int64 if jax.config.jax_enable_x64 else jnp.int32)
        W_bond = jax.random.normal(ks[3], (BOND_DIM, ATOM_DIM * ATOM_DIM), dtype=jnp.float32) * 0.05
        b_bond = jnp.zeros((ATOM_DIM * ATOM_DIM,), dtype=jnp.float32)
        W_ih = jax.random.normal(ks[4], (3 * ATOM_DIM, ATOM_DIM), dtype=jnp.float32) * 0.1
        W_hh = jax.random.normal(ks[5], (3 * ATOM_DIM, ATOM_DIM), dtype=jnp.float32) * 0.1
        b_ih = jnp.zeros((3 * ATOM_DIM,), dtype=jnp.float32)
        b_hh = jnp.zeros((3 * ATOM_DIM,), dtype=jnp.float32)
        return {'atom_features': atom_features, 'bond_features': bond_features, 'pair_indices': pair_indices, 'W_bond': W_bond, 'b_bond': b_bond, 'W_ih': W_ih, 'W_hh': W_hh, 'b_ih': b_ih, 'b_hh': b_hh}
    _L0_gnn_all = _L0_gnn_setup()
    _L0_gnn_in = {k: v for k, v in _L0_gnn_all.items() if k in ('W_bond', 'b_bond', 'W_ih', 'W_hh', 'b_ih', 'b_hh')}
    del _L0_gnn_all

    def _L1_gnn_setup():
        import jax, jax.numpy as jnp
        import numpy as np
        N_NODES = 12500
        N_EDGES = 200000
        D_FEAT = 32
        key = jax.random.key(seed)
        k1, k2, k3 = jax.random.split(key, 3)
        x = jax.random.normal(k1, (N_NODES, D_FEAT), dtype=jnp.float32)
        edge_index = jax.random.randint(k2, (2, N_EDGES), 0, N_NODES, dtype=jnp.int64)
        edge_weight = jax.random.uniform(k3, (N_EDGES,), dtype=jnp.float32)
        return {'x': x, 'edge_index': edge_index, 'edge_weight': edge_weight}
    _L1_gnn_all = _L1_gnn_setup()
    _L1_gnn_in = {k: v for k, v in _L1_gnn_all.items() if k in ()}
    del _L1_gnn_all
    return {'x': x, 'src': src, 'dst': dst, 'edge_attr_16': edge_attr_16, 'edge_weight': edge_weight, 'L0_gnn_W_bond': _L0_gnn_in['W_bond'], 'L0_gnn_b_bond': _L0_gnn_in['b_bond'], 'L0_gnn_W_ih': _L0_gnn_in['W_ih'], 'L0_gnn_W_hh': _L0_gnn_in['W_hh'], 'L0_gnn_b_ih': _L0_gnn_in['b_ih'], 'L0_gnn_b_hh': _L0_gnn_in['b_hh']}

def reference(x, src, dst, edge_attr_16, edge_weight, L0_gnn_W_bond, L0_gnn_b_bond, L0_gnn_W_ih, L0_gnn_W_hh, L0_gnn_b_ih, L0_gnn_b_hh):
    import jax
    import jax.numpy as jnp

    def _L0_gnn_ref(atom_features, bond_features, pair_indices, W_bond, b_bond, W_ih, W_hh, b_ih, b_hh):
        import jax, jax.numpy as jnp
        import numpy as np
        N_ATOMS = 12500
        N_EDGES = 37500
        ATOM_DIM = 32
        BOND_DIM = 16
        STEPS = 4

        def _gru_cell(x, h, W_ih, W_hh, b_ih, b_hh):
            gi = x @ W_ih.T + b_ih
            gh = h @ W_hh.T + b_hh
            i_r, i_z, i_n = jnp.split(gi, 3, axis=-1)
            h_r, h_z, h_n = jnp.split(gh, 3, axis=-1)
            r = jax.nn.sigmoid(i_r + h_r)
            z = jax.nn.sigmoid(i_z + h_z)
            n = jnp.tanh(i_n + r * h_n)
            return (1.0 - z) * n + z * h
        n_atoms, d = atom_features.shape
        edge_mats = (bond_features @ W_bond + b_bond).reshape(-1, d, d)
        dst = pair_indices[:, 0]
        nbr = pair_indices[:, 1]
        h = atom_features
        for _ in range(STEPS):
            msg = jnp.einsum('eij,ej->ei', edge_mats, h[nbr])
            agg = jax.ops.segment_sum(msg, dst, num_segments=n_atoms)
            h = _gru_cell(agg, h, W_ih, W_hh, b_ih, b_hh)
        return h

    def _L1_gnn_ref(x, edge_index, edge_weight):
        import jax, jax.numpy as jnp
        import numpy as np
        N_NODES = 12500
        N_EDGES = 200000
        D_FEAT = 32
        num_nodes = x.shape[0]
        row, col = (edge_index[0], edge_index[1])
        deg = jax.ops.segment_sum(jnp.ones_like(edge_weight), col, num_segments=num_nodes)
        deg_inv_sqrt = jnp.where(deg > 0, jax.lax.rsqrt(deg), 0.0)
        norm = deg_inv_sqrt[row] * edge_weight * deg_inv_sqrt[col]
        msgs = x[row] * norm[:, None]
        out = jax.ops.segment_sum(msgs, col, num_segments=num_nodes)
        return out
    edge_index = jnp.stack([src, dst])
    edge_index_t = jnp.stack([src, dst], axis=1)
    h = jnp.maximum(_layernorm(x, axis=-1), 0.0)
    x = x + _L0_gnn_ref(h, edge_attr_16, edge_index_t, L0_gnn_W_bond, L0_gnn_b_bond, L0_gnn_W_ih, L0_gnn_W_hh, L0_gnn_b_ih, L0_gnn_b_hh)
    h = jnp.maximum(_layernorm(x, axis=-1), 0.0)
    x = x + _L1_gnn_ref(h, edge_index, edge_weight)
    return x

_drawn_inputs = setup_inputs


def setup_inputs(seed=0):
    import zlib

    import numpy as np

    out = dict(_drawn_inputs(seed))
    spreads = {'L0_gnn_b_bond': (0.0, 0.1), 'L0_gnn_b_ih': (0.0, 0.1), 'L0_gnn_b_hh': (0.0, 0.1)}
    factors = {}
    for name, (base, spread) in spreads.items():
        noise = np.random.default_rng([zlib.crc32(name.encode()), seed]).standard_normal(out[name].shape)
        drawn = base * np.exp(spread * noise) if base else spread * noise
        out[name] = jnp.asarray(drawn.astype(out[name].dtype))
    for name, factor in factors.items():
        out[name] = (out[name] * factor).astype(out[name].dtype)
    return out
```

```python
from contextlib import ExitStack

import concourse.bass as bass
from concourse import mybir

F32 = mybir.dt.float32
BF16 = mybir.dt.bfloat16
I32 = mybir.dt.int32
ALU = mybir.AluOpType
ACT = mybir.ActivationFunctionType
AX = mybir.AxisListType

P = 128
STEPS = 4
CH = 8
NQ = 4
QP = P // NQ
CPT = QP // CH
J1 = 25
J2 = 16
J3 = 32
GB = 7
BIG = 1 << 23
EPS = 1e-5

W_ONE, W_DST, W_LO_S, W_WEIGHT, W_POS_D, W_LO_D, W2 = 16, 17, 18, 19, 20, 21, 22
W3 = 18
K1 = 17


def up(a, b):
    return -(-a // b) * b


class Chain:

    def __init__(self, engine, sem, base=0):
        self.engine, self.sem, self.base, self.n = engine, sem, base, 0

    def __call__(self, instruction):
        instruction.then_inc(self.sem, 1)
        self.n += 1
        self.engine.wait_ge(self.sem, self.base + self.n)


def pairs(engine, total, body):
    with engine.Fori(0, total // 2) as i:
        body(i * 2, 0, i)
        body(i * 2 + 1, 1, i)
    if total % 2:
        body(total - 1, 0, total // 2)


def gnn_program(nc, x, src, dst, attr, weight, w_bond, b_bond, w_ih, w_hh, b_ih, b_hh, out):
    N, D = x.shape
    E = src.shape[0]
    KA = attr.shape[1]
    assert D == 32 and KA == 16 and E % (P * J1) == 0
    HB = up(N, P) // P
    HG = up(HB, GB)
    NG = HG // GB
    T1 = E // P
    IT1 = T1 // J1
    T2 = up(T1 + HB, 2 * J2)
    IT2 = T2 // J2
    T3 = up(-(-(E + N * (CH - 1)) // P), 2 * J3)
    IT3 = T3 // J3
    QS = T3 * QP
    QC = QS // CH
    NCH = NQ * QC
    FULL = N // P
    REST = N - FULL * P
    NT = J3 * CPT
    assert T3 * P < BIG and T2 * P < BIG and HB <= P and HB * D <= 7 * 512 and NT == P and T2 % 4 == 0

    r2 = nc.dram_tensor("edges_by_bucket", [T2 * P, W2], F32).ap()
    r3 = nc.dram_tensor("edges_by_node", [T3 * P, W3], F32).ap()
    m2 = nc.dram_tensor("messages_by_bucket", [T2 * P, D + 1], F32).ap()
    st = nc.dram_tensor("chunk_sums", [NCH, D], F32).ap()
    ht = nc.dram_tensor("h_table", [HG * P, D], F32).ap()
    flags = nc.dram_tensor("carry_flags", [NCH, 1], F32).ap()

    outer = ExitStack()
    with outer:
        def sem(name):
            return outer.enter_context(nc.semaphore(name))

        def alloc(stack):
            def sb(name, shape, dt=F32):
                return stack.enter_context(nc.sbuf_tensor(name, shape, dt))

            def pb(name, shape, dt=F32):
                return stack.enter_context(nc.psum_tensor(name, shape, dt))
            return sb, pb

        sb, _ = alloc(outer)
        iota_b = sb("iota_b", [P, P], BF16)
        iota1_b = sb("iota1_b", [P, P], BF16)
        iota1_f = sb("iota1_f", [P, P])
        part_f = sb("part_f", [P, 1])
        ident_f = sb("ident_f", [P, P])
        ident_b = sb("ident_b", [P, P], BF16)
        before_f = sb("before_f", [P, P])
        before_b = sb("before_b", [P, P], BF16)
        ones_f = sb("ones_f", [P, P])
        ones_b = sb("ones_b", [P, P], BF16)
        zrow = sb("zrow", [P, 1])
        pack_s = sb("pack_s", [1, T2 // 4], I32)
        pack_d = sb("pack_d", [1, T2 // 4], I32)
        node_s = sb("node_s", [P, P])
        node_d = sb("node_d", [P, P])
        last_chunk = sb("last_chunk", [P, HG], I32)
        has_edges = sb("has_edges", [P, HG])
        spans = sb("spans_quarter_end", [P, NQ - 1, HG])
        flag_at = sb("flag_at", [P, HB], I32)
        s_cv = sem("vector_chain")
        steps_v = [0]

        s_seen = sem("waits_seen")

        def hold(engine):
            engine.sem_inc(s_seen, 1)

        def hi_registers(eng, pack, word):
            w = eng.value_load(pack[0:1, bass.ds(word, 1)], min_val=0, max_val=(1 << 28) - 1)
            return [nc.s_assert_within((w // (1 << (7 * k))) % 128, 0, HB - 1,
                                       skip_runtime_bounds_check_because="buckets are numbered below HB")
                    for k in range(4)]

        sort = ExitStack()
        with sort:
            sb, pb = alloc(sort)
            lo_s = sb("lo_s", [P, IT1, J1], BF16)
            hi_s = sb("hi_s", [P, IT1, J1], BF16)
            lo_d = sb("lo_d", [P, IT1, J1], BF16)
            hi_d = sb("hi_d", [P, IT1, J1], BF16)
            off_s = sb("offset_src", [P, T1])
            off_d = sb("offset_dst", [P, T1])
            totals = sb("totals", [P, 2])

            s_keys = sem("keys_loaded")
            s_iota = sem("iotas_made")
            s_const = sem("constants_made")
            s_split = sem("keys_split")
            s_stg = sem("keys_staged_g")
            s_oh_v = sem("onehots_by_vector")
            s_oh_g = sem("onehots_by_gpsimd")
            s_cnt = sem("counts_in_psum")
            s_cev = sem("counts_copied")
            s_zero = sem("zeros_made")
            s_fill = sem("tables_cleared")

            with ExitStack() as c1:
                sb, pb = alloc(c1)
                oh = [sb(f"onehots_{b}", [P, J1, 4, P], BF16) for b in range(2)]
                kst = [sb(f"key_stage_{b}", [P, 4, J1]) for b in range(2)]
                cnt_s = sb("count_src", [P, T1])
                cnt_d = sb("count_dst", [P, T1])
                key_i = sb("key_i", [P, IT1, J1], I32)
                iota_f = sb("iota_f", [P, P])
                iota_i = sb("iota_i", [P, P], I32)
                part_i = sb("part_i", [P, 1], I32)
                pcnt = [pb(f"pcnt{b}", [P, 2, J1]) for b in range(2)]
                pnode_s = pb("pnode_s", [P, P])
                pnode_d = pb("pnode_d", [P, P])
                block = c1.enter_context(nc.Block())
                zeros = oh[0][:].rearrange("p a b c -> p (a b c)").bitcast(F32)

                @block.sync
                def _(sp):
                    sp.dma_start(key_i[:], src.rearrange("(i p u) -> p i u", p=P, u=J1)).then_inc(s_keys, 16)
                    sp.wait_ge(s_zero, 1)
                    n, width = 0, J1 * 2 * P
                    for table in (r2, r3, m2):
                        flat = table.rearrange("(p a) w -> p (a w)", p=P)
                        for at in range(0, flat.shape[1], width):
                            m = min(width, flat.shape[1] - at)
                            sp.dma_start(flat[:, at:at + m], zeros[:, 0:m]).then_inc(s_fill, 16)
                            n += 1
                    sp.dma_start(flags.rearrange("(p a) w -> p (a w)", p=P),
                                 cnt_s[:, 0:NCH // P]).then_inc(s_fill, 16)
                    sp.wait_ge(s_split, 1)
                    sp.dma_start(key_i[:], dst.rearrange("(i p u) -> p i u", p=P, u=J1)).then_inc(s_keys, 16)
                    sp.wait_ge(s_fill, 16 * (n + 1))
                    sp.sem_inc(s_zero, 1)

                @block.gpsimd
                def _(pool):
                    pool.iota(iota_i[:], [[1, P]], base=0, channel_multiplier=0).then_inc(s_iota, 1)
                    pool.iota(part_i[:], [[1, 1]], base=0, channel_multiplier=1).then_inc(s_iota, 1)
                    pool.wait_ge(s_split, 2)
                    pool.wait_ge(s_zero, 2)

                    def build(it, b, i):
                        pool.wait_ge(s_cnt, it + 1)
                        hold(pool)
                        pool.tensor_copy(kst[b][:, 2, :], hi_d[:, bass.ds(it, 1), :].rearrange("p a u -> p (a u)")).then_inc(s_stg, 1)
                        pool.tensor_copy(kst[b][:, 3, :], lo_d[:, bass.ds(it, 1), :].rearrange("p a u -> p (a u)")).then_inc(s_stg, 1)
                        pool.wait_ge(s_stg, it * 2 + 2)
                        hold(pool)
                        for u in range(J1):
                            for k in (2, 3):
                                last = pool.tensor_scalar(oh[b][:, u, k, :], iota_b[:], kst[b][:, k, u:u + 1], None, ALU.is_equal)
                        last.then_inc(s_oh_g, 1)
                    pairs(pool, IT1, build)

                @block.vector
                def _(dve):
                    ch = Chain(dve, s_cv, steps_v[0])
                    ch(dve.memset(zeros, 0.0))
                    ch(dve.memset(cnt_s[:, 0:NCH // P], 1.0))
                    dve.sem_inc(s_zero, 1)
                    dve.wait_ge(s_iota, 2)
                    ch(dve.tensor_copy(iota_f[:], iota_i[:]))
                    ch(dve.tensor_copy(iota_b[:], iota_i[:]))
                    ch(dve.tensor_copy(part_f[:], part_i[:]))
                    ch(dve.tensor_scalar(iota1_f[:], iota_f[:], 1.0, None, ALU.add))
                    ch(dve.tensor_copy(iota1_b[:], iota1_f[:]))
                    ch(dve.tensor_scalar(ident_f[:], iota_f[:], part_f[:, 0:1], None, ALU.is_equal))
                    ch(dve.tensor_copy(ident_b[:], ident_f[:]))
                    ch(dve.tensor_scalar(before_f[:], iota_f[:], part_f[:, 0:1], None, ALU.is_gt))
                    ch(dve.tensor_copy(before_b[:], before_f[:]))
                    ch(dve.memset(ones_f[:], 1.0))
                    ch(dve.memset(ones_b[:], 1.0))
                    ch(dve.memset(zrow[:], 0.0))
                    ch(dve.memset(oh[1][:, 0, 0, :], 0.0))
                    dve.sem_inc(s_const, 1)
                    tmp = cnt_d[:].bitcast(I32).rearrange("p (a b) -> p a b", b=J1)
                    for n, (hi, lo) in enumerate(((hi_s, lo_s), (hi_d, lo_d))):
                        dve.wait_ge(s_keys, 16 * (n + 1))
                        ch(dve.tensor_scalar(tmp, key_i[:], 7, None, ALU.logical_shift_right))
                        ch(dve.tensor_copy(hi[:], tmp))
                        ch(dve.tensor_scalar(tmp, key_i[:], 127, None, ALU.bitwise_and))
                        ch(dve.tensor_copy(lo[:], tmp))
                        dve.sem_inc(s_split, 1)
                    dve.wait_ge(s_zero, 2)
                    base = steps_v[0] + ch.n

                    def build(it, b, i):
                        dve.wait_ge(s_cnt, it + 1)
                        st_ = Chain(dve, s_cv, it * 2 + base)
                        st_(dve.tensor_copy(kst[b][:, 0, :], hi_s[:, bass.ds(it, 1), :].rearrange("p a u -> p (a u)")))
                        st_(dve.tensor_copy(kst[b][:, 1, :], lo_s[:, bass.ds(it, 1), :].rearrange("p a u -> p (a u)")))
                        for u in range(J1):
                            for k in (0, 1):
                                last = dve.tensor_scalar(oh[b][:, u, k, :], iota_b[:], kst[b][:, k, u:u + 1], None, ALU.is_equal)
                        last.then_inc(s_oh_v, 1)
                    pairs(dve, IT1, build)
                    ch.n += 2 * IT1
                    dve.wait_ge(s_cev, IT1 + 2)
                    one = ones_f[:, 0:1].broadcast_to([P, T1])
                    ch(dve.tensor_tensor_scan(off_s[:], one, cnt_s[:], 0.0, ALU.mult, ALU.add))
                    ch(dve.tensor_tensor_scan(off_d[:], one, cnt_d[:], 0.0, ALU.mult, ALU.add))
                    ch(dve.tensor_copy(totals[:, 0:1], off_s[:, T1 - 1:T1]))
                    ch(dve.tensor_copy(totals[:, 1:2], off_d[:, T1 - 1:T1]))
                    ch(dve.tensor_tensor(off_s[:], off_s[:], cnt_s[:], ALU.subtract))
                    ch(dve.tensor_tensor(off_d[:], off_d[:], cnt_d[:], ALU.subtract))
                    ch(dve.tensor_copy(node_s[:], pnode_s[:]))
                    ch(dve.tensor_copy(node_d[:], pnode_d[:]))
                    steps_v[0] += ch.n

                @block.scalar
                def _(act):
                    act.sem_inc(s_cev, 2)
                    act.wait_ge(s_split, 2)
                    act.wait_ge(s_zero, 2)

                    def copy(it, b, i):
                        act.wait_ge(s_cnt, it + 3)
                        act.copy(cnt_s[:, bass.ds(it * J1, J1)], pcnt[b][:, 0, :])
                        act.copy(cnt_d[:, bass.ds(it * J1, J1)], pcnt[b][:, 1, :]).then_inc(s_cev, 1)
                    pairs(act, IT1, copy)

                @block.tensor
                def _(pe):
                    pe.wait_ge(s_const, 1)
                    for acc in (pnode_s, pnode_d):
                        clear = pe.matmul(acc[:], oh[1][:, 0, 0, :], ones_b[:], start=True, stop=False, skip_group_check=True)
                    clear.then_inc(s_cnt, 2)

                    def count(it, b, i):
                        pe.wait_ge(s_oh_v, it + 1)
                        pe.wait_ge(s_oh_g, it + 1)
                        pe.wait_ge(s_cev, it + 1)
                        for u in range(J1):
                            for k, acc in enumerate((pnode_s, pnode_d)):
                                hi, lo = oh[b][:, u, 2 * k, :], oh[b][:, u, 2 * k + 1, :]
                                pe.matmul(pcnt[b][:, k, u:u + 1], hi, ones_b[:, 0:1], start=True, stop=True)
                                last = pe.matmul(acc[:], lo, hi, start=False, stop=False, skip_group_check=True)
                        last.then_inc(s_cnt, 1)
                    pairs(pe, IT1, count)

            plan = ExitStack()
            sort.enter_context(plan)
            sb, _ = alloc(plan)
            keep = sb("same_bucket", [P, T2])
            off_n = sb("offset_node", [P, T2])
            s_io2 = sem("tile_numbers")
            s_pv = sem("sums_wanted")
            s_pp = sem("sums_in_psum")
            with ExitStack() as c2:
                sb, pb = alloc(c2)
                tile_i = sb("tile_i", [P, T2], I32)
                tile_f = sb("tile_f", [P, T2])
                at_or_after = sb("at_or_after", [P, T2], BF16)
                hi_t = sb("bucket_of_tile", [P, T2])
                hot = sb("bucket_onehot", [P, T2])
                tint = sb("tint", [P, 2], I32)
                ntiles = sb("ntiles", [P, 2])
                tb = sb("bucket_tile", [P, 2])
                ni = sb("ni", [P, HB], I32)
                nchunk = sb("nchunk", [P, HB])
                first = sb("first_chunk", [P, HB])
                colsum = sb("colsum", [P, HB])
                slots = sb("slots", [P, HB])
                slots_t = sb("slots_t", [P, P])
                ps = pb("plan_psum", [P, 512])
                block = c2.enter_context(nc.Block())
                spans_of = [(a, min(512, T2 - a)) for a in range(0, T2, 512)]

                @block.gpsimd
                def _(pool):
                    pool.iota(tile_i[:], [[1, T2]], base=0, channel_multiplier=0).then_inc(s_io2, 1)

                asked = [0]
                jobs = []

                @block.vector
                def _(dve):
                    ch = Chain(dve, s_cv, steps_v[0])

                    def product(*job):
                        jobs.append(job)
                        dve.sem_inc(s_pv, 1)
                        asked[0] += 1
                        dve.wait_ge(s_pp, asked[0])

                    ch(dve.tensor_scalar(tint[:], totals[:], float(P - 1), None, ALU.add))
                    ch(dve.tensor_scalar(tint[:], tint[:], 7, None, ALU.logical_shift_right))
                    ch(dve.tensor_copy(ntiles[:], tint[:]))
                    product(ps[:, 0:2], before_f[:], ntiles[:])
                    ch(dve.tensor_copy(tb[:], ps[:, 0:2]))
                    for k, off in enumerate((off_s, off_d)):
                        ch(dve.tensor_scalar(ntiles[:, k:k + 1], tb[:, k:k + 1], float(P), None, ALU.mult))
                        ch(dve.tensor_scalar(off[:], off[:], ntiles[:, k:k + 1], None, ALU.add))
                    dve.wait_ge(s_io2, 1)
                    ch(dve.tensor_copy(tile_f[:], tile_i[:]))
                    for k, pack in ((1, pack_d), (0, pack_s)):
                        ch(dve.tensor_scalar(at_or_after[:], tile_f[:], tb[:, k:k + 1], None, ALU.is_ge))
                        for a, m in spans_of:
                            product(ps[:, 0:m], ones_b[0:HB, :], at_or_after[0:HB, a:a + m])
                            ch(dve.tensor_scalar(hi_t[:, a:a + m], ps[:, 0:m], -1.0, None, ALU.add))
                        ch(dve.tensor_copy(tile_i[0:1, :], hi_t[0:1, :]))
                        four = tile_i[0:1, :].rearrange("p (w k) -> p w k", k=4)
                        for j in (1, 2, 3):
                            ch(dve.tensor_scalar(four[:, :, j], four[:, :, j], 7 * j, None, ALU.logical_shift_left))
                            ch(dve.tensor_tensor(four[:, :, 0], four[:, :, 0], four[:, :, j], ALU.bitwise_or))
                        ch(dve.tensor_copy(pack[:].bitcast(F32), four[:, :, 0].bitcast(F32)))
                    ch(dve.memset(keep[:, 0:1], 0.0))
                    ch(dve.tensor_tensor(keep[:, 1:T2], hi_t[:, 1:T2], hi_t[:, 0:T2 - 1], ALU.is_equal))
                    nd = node_s[:, 0:HB]
                    ch(dve.tensor_scalar(ni[:], nd, float(CH - 1), None, ALU.add))
                    ch(dve.tensor_scalar(ni[:], ni[:], CH.bit_length() - 1, None, ALU.logical_shift_right))
                    ch(dve.tensor_copy(nchunk[:], ni[:]))
                    product(ps[:, 0:HB], ones_f[:], nchunk[:])
                    ch(dve.tensor_copy(colsum[:], ps[:, 0:HB]))
                    one = ones_f[:, 0:1].broadcast_to([P, HB])
                    ch(dve.tensor_tensor_scan(first[:], one, colsum[:], 0.0, ALU.mult, ALU.add))
                    ch(dve.tensor_tensor(first[:], first[:], colsum[:], ALU.subtract))
                    product(ps[:, 0:HB], before_f[:], nchunk[:])
                    ch(dve.tensor_tensor(first[:], first[:], ps[:, 0:HB], ALU.add))
                    ch(dve.memset(has_edges[:], 0.0))
                    ch(dve.memset(last_chunk[:], 0))
                    ch(dve.memset(spans[:], 0.0))
                    ch(dve.tensor_scalar(has_edges[:, 0:HB], nd, 0.5, None, ALU.is_gt))
                    ch(dve.tensor_tensor(slots[:], first[:], nchunk[:], ALU.add))
                    ch(dve.tensor_scalar(slots[:], slots[:], -1.0, 0.0, ALU.add, ALU.max))
                    ch(dve.tensor_copy(last_chunk[:, 0:HB], slots[:]))
                    for q in range(NQ - 1):
                        s = spans[:, q, 0:HB]
                        ch(dve.scalar_tensor_tensor(out=s, in0=slots[:], scalar=float(QC * (q + 1)), in1=has_edges[:, 0:HB],
                                                    op0=ALU.is_ge, op1=ALU.mult))
                        ch(dve.scalar_tensor_tensor(out=s, in0=first[:], scalar=float(QC * (q + 1)), in1=s,
                                                    op0=ALU.is_lt, op1=ALU.mult))
                    ch(dve.tensor_scalar(slots[:], has_edges[:, 0:HB], -float(BIG), float(BIG), ALU.mult, ALU.add))
                    ch(dve.tensor_tensor(slots[:], slots[:], first[:], ALU.add))
                    ch(dve.tensor_copy(flag_at[:], slots[:]))
                    ch(dve.tensor_scalar(slots[:], first[:], float(CH), None, ALU.mult))
                    product("transpose", ps[0:HB, 0:P], slots[:])
                    ch(dve.tensor_copy(slots_t[0:HB, :], ps[0:HB, 0:P]))
                    ch(dve.tensor_scalar(hot[:], hi_t[:], part_f[:, 0:1], None, ALU.is_equal))
                    for a, m in spans_of:
                        product(ps[:, 0:m], slots_t[0:HB, :], hot[0:HB, a:a + m])
                        ch(dve.tensor_copy(off_n[:, a:a + m], ps[:, 0:m]))
                    steps_v[0] += ch.n

                @block.tensor
                def _(pe):
                    for n, job in enumerate(jobs):
                        pe.wait_ge(s_pv, n + 1)
                        if job[0] == "transpose":
                            pe.transpose(job[1], job[2], ident_f[:]).then_inc(s_pp, 1)
                        else:
                            pe.matmul(job[0], job[1], job[2], start=True, stop=True).then_inc(s_pp, 1)

            def rank_engines(name, stack, U, credits_from_pairs=None):
                sb, pb = alloc(stack)
                r = {}
                r["U"], r["groups"] = U, [(a, min(a + 4, U)) for a in range(0, U, 4)]
                r["O"] = [sb(f"{name}_onehot{b}", [P, U, P], BF16) for b in range(2)]
                r["OT"] = [sb(f"{name}_onehot_t{b}", [P, 4, P]) for b in range(2)]
                r["off"] = [sb(f"{name}_off{b}", [P, U]) for b in range(2)]
                r["rk"] = [sb(f"{name}_rank{b}", [P, U]) for b in range(2)]
                r["X"] = [pb(f"{name}_x{b}", [P, 4, P]) for b in range(2)]
                r["PT"] = [pb(f"{name}_pt{b}", [P, 8, P], BF16) for b in range(2)]
                r["pos"] = [pb(f"{name}_pos{b}", [P, 512]) for b in range(2)]
                for s in ("o", "ot", "otc", "n1", "xfree", "pos", "math"):
                    r["s_" + s] = sem(f"{name}_{s}")
                return r

            def rank_tensor(pe, r):
                G = len(r["groups"])
                pe.sem_inc(r["s_n1"], 2)
                pe.sem_inc(r["s_pos"], 2)

                def offsets(it, b, g):
                    a, z = r["groups"][g]
                    pe.wait_ge(r["s_otc"], it * G + g + 3)
                    for u in range(a, z):
                        last = pe.matmul(r["pos"][b][:, u:u + 1], r["OT"][(b * G + g) % 2][:, u - a, :],
                                         r["off"][b][:, u:u + 1], start=True, stop=True)
                    last.then_inc(r["s_n1"], 1)

                def body(it, b, i):
                    pe.wait_ge(r["s_math"], it + 1)
                    for g, (a, z) in enumerate(r["groups"]):
                        ring = (b * G + g) % 2
                        pe.wait_ge(r["s_o"], it * G + g + 1)
                        pe.wait_ge(r["s_xfree"], it * G + g + 1)
                        pe.matmul(r["X"][ring][:, 0:z - a, :], before_b[:], r["O"][b][:, a:z, :], start=True, stop=True)
                        pe.wait_ge(r["s_otc"], it * G + g + 1)
                        for u in range(a, z):
                            last = pe.transpose(r["PT"][ring][:, u - a, :], r["O"][b][:, u, :], ident_b[:])
                        last.then_inc(r["s_ot"], 1)
                        if g:
                            offsets(it, b, g - 1)
                    offsets(it, b, G - 1)
                    pe.wait_ge(r["s_n1"], it * G + G + 2)
                    pe.sem_inc(r["s_pos"], 1)
                return body

            def rank_scalar(act, r):
                G = len(r["groups"])
                act.sem_inc(r["s_otc"], 2)

                def body(it, b):
                    for g, (a, z) in enumerate(r["groups"]):
                        ring = (b * G + g) % 2
                        act.wait_ge(r["s_ot"], it * G + g + 1)
                        act.wait_ge(r["s_n1"], it * G + g + 1)
                        act.copy(r["OT"][ring][:, 0:z - a, :], r["PT"][ring][:, 0:z - a, :]).then_inc(r["s_otc"], 1)
                return body

            def rank_vector(dve, r, iota, key):
                G = len(r["groups"])
                dve.sem_inc(r["s_xfree"], 2)
                dve.sem_inc(r["s_math"], 2)

                def build(b, g):
                    a, z = r["groups"][g]
                    for u in range(a, z):
                        last = dve.tensor_scalar(r["O"][b][:, u, :], iota, key(b, u), None, ALU.is_equal)
                    last.then_inc(r["s_o"], 1)

                def body(it, b):
                    build(b, 0)
                    build(b, 1)
                    for g, (a, z) in enumerate(r["groups"]):
                        if g + 2 < G:
                            build(b, g + 2)
                        dve.wait_ge(r["s_ot"], it * G + g + 1)
                        for u in range(a, z):
                            o = r["O"][b][:, u, :]
                            last = dve.tensor_tensor_reduce(out=o, in0=r["X"][(b * G + g) % 2][:, u - a, :], in1=o,
                                                            scale=1.0, scalar=0.0, op0=ALU.mult, op1=ALU.add,
                                                            accum_out=r["rk"][b][:, u:u + 1])
                        last.then_inc(r["s_xfree"], 1)
                    dve.wait_ge(r["s_xfree"], it * G + G + 2)
                    dve.wait_ge(r["s_pos"], it + 3)
                return body

            s_ld1 = [sem(f"edges_loaded{b}") for b in range(2)]
            s_row = sem("rows_made")
            s_sc1 = [sem(f"rows_scattered{b}") for b in range(2)]
            s_v1 = sem("pass1_chain")
            LJ = J2.bit_length() - 1
            with ExitStack() as c3:
                r = rank_engines("p1", c3, 2 * J1)
                sb, pb = alloc(c3)
                at_ = [sb(f"attr{b}", [P, J1, KA]) for b in range(2)]
                wt = [sb(f"weight{b}", [P, J1]) for b in range(2)]
                di = [sb(f"dst{b}", [P, J1], I32) for b in range(2)]
                key = [sb(f"key1_{b}", [P, 2 * J1]) for b in range(2)]
                row = [sb(f"row{b}", [P, J1, W2]) for b in range(2)]
                pi = [sb(f"place_i{b}", [P, 2 * J1], I32) for b in range(2)]
                pj = sb("place_j", [P, 2 * J1], I32)
                pk = sb("place_k", [P, 2 * J1], I32)
                block = c3.enter_context(nc.Block())

                @block.sync
                def _(sp):
                    def load(it, b, i):
                        sp.wait_ge(s_row, it + 1)
                        e = bass.ds(it * (P * J1), P * J1)
                        sp.dma_start(at_[b][:], attr[e, :].rearrange("(p u) k -> p u k", p=P)).then_inc(s_ld1[b], 16)
                        sp.dma_start(wt[b][:], weight[e].rearrange("(p u) -> p u", p=P)).then_inc(s_ld1[b], 16)
                        sp.dma_start(di[b][:], dst[e].rearrange("(p u) -> p u", p=P)).then_inc(s_ld1[b], 16)
                    pairs(sp, IT1, load)

                @block.tensor
                def _(pe):
                    pairs(pe, IT1, rank_tensor(pe, r))

                @block.scalar
                def _(act):
                    act.sem_inc(s_row, 2)
                    evac = rank_scalar(act, r)

                    def body(it, b, i):
                        evac(it, b)
                        act.wait_ge(s_ld1[b], i * 48 + 48)
                        act.wait_ge(s_sc1[b], i * (16 * J1))
                        act.copy(row[b][:, :, 0:KA], at_[b][:])
                        act.copy(row[b][:, :, W_WEIGHT], wt[b][:])
                        act.copy(row[b][:, :, W_DST].bitcast(I32), di[b][:])
                        act.add(row[b][:, :, W_LO_S], lo_s[:, bass.ds(it, 1), :].rearrange("p a u -> p (a u)"), 1.0)
                        act.add(row[b][:, :, W_LO_D], lo_d[:, bass.ds(it, 1), :].rearrange("p a u -> p (a u)"), 1.0).then_inc(s_row, 1)
                    pairs(act, IT1, body)

                @block.vector
                def _(dve):
                    K = 10
                    c0 = Chain(dve, s_v1)
                    c0(dve.memset(row[0][:, :, W_ONE], 1.0))
                    c0(dve.memset(row[1][:, :, W_ONE], 1.0))
                    ranks = rank_vector(dve, r, iota_b[:], lambda b, u: key[b][:, u:u + 1])

                    def body(it, b, i):
                        dve.wait_ge(r["s_math"], it + 1)
                        dve.wait_ge(r["s_pos"], it + 1)
                        ch = Chain(dve, s_v1, it * K + 2)
                        for k, (hi, off) in enumerate(((hi_s, off_s), (hi_d, off_d))):
                            ch(dve.tensor_copy(key[b][:, k * J1:(k + 1) * J1], hi[:, bass.ds(it, 1), :].rearrange("p a u -> p (a u)")))
                            ch(dve.tensor_copy(r["off"][b][:, k * J1:(k + 1) * J1], off[:, bass.ds(it * J1, J1)]))
                        ranks(it, b)
                        dve.wait_ge(s_sc1[b], i * (16 * J1))
                        p_ = pi[b][:]
                        ch(dve.tensor_tensor(p_, r["pos"][b][:, 0:2 * J1], r["rk"][b][:], ALU.add))
                        ch(dve.tensor_scalar(pj[:], p_, 7, J2 - 1, ALU.logical_shift_right, ALU.bitwise_and))
                        ch(dve.tensor_scalar(pk[:], p_, P - 1, LJ, ALU.bitwise_and, ALU.logical_shift_left))
                        ch(dve.tensor_tensor(pj[:], pj[:], pk[:], ALU.bitwise_or))
                        ch(dve.tensor_scalar(p_, p_, 7 + LJ, 7 + LJ, ALU.logical_shift_right, ALU.logical_shift_left))
                        ch(dve.tensor_tensor(p_, p_, pj[:], ALU.bitwise_or))
                        assert ch.n == K
                        dve.tensor_copy(row[b][:, :, W_POS_D], pi[b][:, J1:2 * J1].bitcast(F32)).then_inc(r["s_math"], 1)
                    pairs(dve, IT1, body)

                @block.gpsimd
                def _(pool):
                    def scatter(it, b, i):
                        pool.wait_ge(s_row, it + 3)
                        pool.wait_ge(r["s_math"], it + 3)
                        hold(pool)
                        for u in range(J1):
                            pool.indirect_dma_start(
                                out=r2, out_offset=bass.IndirectOffsetOnAxis(ap=pi[b][:, u:u + 1], axis=0),
                                in_=row[b][:, u, :], in_offset=None).then_inc(s_sc1[b], 16)
                    pairs(pool, IT1, scatter)
                    pool.wait_ge(s_sc1[0], 16 * J1 * ((IT1 + 1) // 2))
                    pool.wait_ge(s_sc1[1], 16 * J1 * (IT1 // 2))

            s_ld2 = [sem(f"r2_loaded{b}") for b in range(2)]
            s_o2 = sem("onehots_2")
            s_c2 = sem("counts_2")
            s_e2 = sem("counts_2_copied")
            tiles2 = r2.rearrange("(i p u) w -> i p (u w)", p=P, u=J2)
            with ExitStack() as c4:
                sb, pb = alloc(c4)
                rec = [sb(f"rec2_{b}", [P, J2, W2]) for b in range(2)]
                oh2 = [sb(f"oh2_{b}", [P, J2, P], BF16) for b in range(2)]
                cnt = sb("count_node", [P, T2])
                acc = sb("count_scan", [P, T2])
                pc = [pb(f"pc2_{b}", [P, J2]) for b in range(2)]
                block = c4.enter_context(nc.Block())

                @block.sync
                def _(sp):
                    def load(it, b, i):
                        sp.wait_ge(s_o2, it + 1)
                        sp.dma_start(rec[b][:], tiles2[bass.ds(it, 1)].rearrange("a p w -> (a p) w")).then_inc(s_ld2[b], 16)
                    pairs(sp, IT2, load)

                @block.vector
                def _(dve):
                    dve.sem_inc(s_o2, 2)

                    def build(it, b, i):
                        dve.wait_ge(s_ld2[b], i * 16 + 16)
                        dve.wait_ge(s_c2, it + 1)
                        for u in range(J2):
                            last = dve.tensor_scalar(oh2[b][:, u, :], iota1_b[:], rec[b][:, u, W_LO_S:W_LO_S + 1], None, ALU.is_equal)
                        last.then_inc(s_o2, 1)
                    pairs(dve, IT2, build)
                    dve.wait_ge(s_e2, IT2 + 2)
                    ch = Chain(dve, s_cv, steps_v[0])
                    ch(dve.tensor_tensor_scan(acc[:], keep[:], cnt[:], 0.0, ALU.mult, ALU.add))
                    ch(dve.tensor_tensor(acc[:], acc[:], cnt[:], ALU.subtract))
                    ch(dve.tensor_tensor(off_n[:], off_n[:], acc[:], ALU.add))
                    steps_v[0] += ch.n

                @block.tensor
                def _(pe):
                    pe.sem_inc(s_c2, 2)

                    def count(it, b, i):
                        pe.wait_ge(s_o2, it + 3)
                        pe.wait_ge(s_e2, it + 1)
                        for u in range(J2):
                            last = pe.matmul(pc[b][:, u:u + 1], oh2[b][:, u, :], ones_b[:, 0:1], start=True, stop=True)
                        last.then_inc(s_c2, 1)
                    pairs(pe, IT2, count)

                @block.scalar
                def _(act):
                    act.sem_inc(s_e2, 2)

                    def copy(it, b, i):
                        act.wait_ge(s_c2, it + 3)
                        act.copy(cnt[:, bass.ds(it * J2, J2)], pc[b][:]).then_inc(s_e2, 1)
                    pairs(act, IT2, copy)

            s_ld3 = [sem(f"r2_loaded_again{b}") for b in range(2)]
            s_sc2 = [sem(f"edges_scattered{b}") for b in range(2)]
            s_v2 = sem("pass2_chain")
            s_flag = sem("flags_scattered")
            LS = QP.bit_length() - 1
            L3 = J3.bit_length() - 1
            with ExitStack() as c5:
                r = rank_engines("p2", c5, J2)
                sb, pb = alloc(c5)
                rec = [sb(f"rec2b_{b}", [P, J2, W2]) for b in range(2)]
                slot = sb("slot", [P, J2])
                quarter = sb("quarter", [P, J2])
                extra = sb("extra", [P, J2])
                place = [sb(f"place2_{b}", [P, J2], I32) for b in range(2)]
                si = sb("slot_i", [P, J2], I32)
                ti = sb("slot_t", [P, J2], I32)
                block = c5.enter_context(nc.Block())

                @block.sync
                def _(sp):
                    def load(it, b, i):
                        sp.wait_ge(s_sc2[b], i * (16 * J2))
                        sp.dma_start(rec[b][:], tiles2[bass.ds(it, 1)].rearrange("a p w -> (a p) w")).then_inc(s_ld3[b], 16)
                    pairs(sp, IT2, load)

                @block.tensor
                def _(pe):
                    pairs(pe, IT2, rank_tensor(pe, r))

                @block.scalar
                def _(act):
                    evac = rank_scalar(act, r)
                    pairs(act, IT2, lambda it, b, i: evac(it, b))

                @block.vector
                def _(dve):
                    K = 15
                    ranks = rank_vector(dve, r, iota1_b[:], lambda b, u: rec[b][:, u, W_LO_S:W_LO_S + 1])

                    def body(it, b, i):
                        dve.wait_ge(s_ld3[b], i * 16 + 16)
                        dve.wait_ge(r["s_math"], it + 1)
                        dve.wait_ge(r["s_pos"], it + 1)
                        ch = Chain(dve, s_v2, it * K)
                        ch(dve.tensor_copy(r["off"][b][:], off_n[:, bass.ds(it * J2, J2)]))
                        ranks(it, b)
                        ch(dve.tensor_tensor(slot[:], r["pos"][b][:, 0:J2], r["rk"][b][:], ALU.add))
                        ch(dve.tensor_scalar(quarter[:], slot[:], float(QS), None, ALU.is_ge))
                        for q in (2, 3):
                            ch(dve.scalar_tensor_tensor(out=quarter[:], in0=slot[:], scalar=float(q * QS), in1=quarter[:],
                                                        op0=ALU.is_ge, op1=ALU.add))
                        ch(dve.scalar_tensor_tensor(out=si[:], in0=quarter[:], scalar=-float(QS), in1=slot[:],
                                                    op0=ALU.mult, op1=ALU.add))
                        ch(dve.tensor_scalar(extra[:], rec[b][:, :, W_ONE], -float(BIG), float(BIG), ALU.mult, ALU.add))
                        ch(dve.scalar_tensor_tensor(out=extra[:], in0=quarter[:], scalar=float(QP * J3), in1=extra[:],
                                                    op0=ALU.mult, op1=ALU.add))
                        ch(dve.tensor_scalar(ti[:], si[:], LS, J3 - 1, ALU.logical_shift_right, ALU.bitwise_and))
                        ch(dve.tensor_copy(slot[:], ti[:]))
                        ch(dve.tensor_tensor(extra[:], extra[:], slot[:], ALU.add))
                        ch(dve.tensor_scalar(ti[:], si[:], QP - 1, L3, ALU.bitwise_and, ALU.logical_shift_left))
                        ch(dve.tensor_scalar(si[:], si[:], LS + L3, 7 + L3, ALU.logical_shift_right, ALU.logical_shift_left))
                        ch(dve.tensor_tensor(si[:], si[:], ti[:], ALU.bitwise_or))
                        ch(dve.tensor_copy(slot[:], si[:]))
                        assert ch.n == K, ch.n
                        dve.tensor_tensor(place[b][:], slot[:], extra[:], ALU.add).then_inc(r["s_math"], 1)
                    pairs(dve, IT2, body)

                @block.gpsimd
                def _(pool):
                    for h in range(HB):
                        pool.indirect_dma_start(
                            out=flags, out_offset=bass.IndirectOffsetOnAxis(ap=flag_at[:, h:h + 1], axis=0),
                            in_=zrow[:], in_offset=None, bounds_check=NCH - 1, oob_is_err=False).then_inc(s_flag, 16)

                    def scatter(it, b, i):
                        pool.wait_ge(r["s_math"], it + 3)
                        hold(pool)
                        for u in range(J2):
                            pool.indirect_dma_start(
                                out=r3, out_offset=bass.IndirectOffsetOnAxis(ap=place[b][:, u:u + 1], axis=0),
                                in_=rec[b][:, u, 0:W3], in_offset=None,
                                bounds_check=T3 * P - 1, oob_is_err=False).then_inc(s_sc2[b], 16)
                    pairs(pool, IT2, scatter)
                    pool.wait_ge(s_sc2[0], 16 * J2 * (IT2 // 2))
                    pool.wait_ge(s_sc2[1], 16 * J2 * (IT2 // 2))
                    pool.wait_ge(s_flag, 16 * HB)

        lay = ExitStack()
        with lay:
            sb, _ = alloc(lay)
            xs = sb("x_nodes", [P, HG, D])
            cat = sb("agg_h_one", [P, HG, 2 * D + 2])
            wb = sb("w_bond_blocks", [P, K1, P])
            wx = sb("w_gru", [2 * D + 2, 4 * D])
            mask4 = sb("chunk_of_row", [P, CPT])
            gt = sb("g_nodes", [P, HG, D])
            mean = sb("mean", [P, HG])
            var = sb("var", [P, HG])
            dis = sb("deg_inv_sqrt", [P, HG])
            s_x = sem("x_loaded")
            s_xz = sem("x_cleared")
            s_w = sem("weights_loaded")
            s_wz = sem("weights_cleared")
            s_sq = sem("sqrt_wanted")
            s_sqd = sem("sqrt_done")
            s_h0 = sem("h0_stored")

            s_ln = [0]

            def norm_relu(dve, ch, xin, xout, tmp):
                ch(dve.tensor_reduce(mean[:], xin, AX.X, ALU.add))
                ch(dve.tensor_scalar(mean[:], mean[:], 1.0 / D, None, ALU.mult))
                ch(dve.tensor_tensor(tmp, xin, mean[:].unsqueeze(2).broadcast_to([P, HG, D]), ALU.subtract))
                ch(dve.tensor_tensor(xout, tmp, tmp, ALU.mult))
                ch(dve.tensor_reduce(var[:], xout, AX.X, ALU.add))
                ch(dve.tensor_scalar(var[:], var[:], 1.0 / D, EPS, ALU.mult, ALU.add))
                dve.sem_inc(s_sq, 1)
                s_ln[0] += 1
                dve.wait_ge(s_sqd, s_ln[0])
                ch(dve.reciprocal(mean[:], var[:]))
                ch(dve.tensor_tensor(tmp, tmp, mean[:].unsqueeze(2).broadcast_to([P, HG, D]), ALU.mult))
                ch(dve.tensor_scalar(xout, tmp, 0.0, None, ALU.max))

            def node_rows(table, rows):
                return table[0:rows].rearrange("(h l) d -> l h d", l=P)

            with ExitStack() as c6:
                sb, pb = alloc(c6)
                wl = sb("w_bond_rows", [P, K1, D])
                wlt = sb("w_bond_cols", [P, K1, D])
                wg = sb("w_gru_rows", [2 * D, 3, D])
                wgt = sb("w_gru_cols", [2 * D, 3, D])
                tmp = sb("ln_tmp", [P, HG, D])
                pn = sb("pn", [P, 1])
                pni = sb("pni", [P, 1], I32)
                block = c6.enter_context(nc.Block())

                @block.sync
                def _(sp):
                    sp.wait_ge(s_xz, 1)
                    n = 1
                    sp.dma_start(xs[:, 0:FULL, :], node_rows(x, FULL * P)).then_inc(s_x, 16)
                    if REST:
                        sp.dma_start(xs[0:REST, FULL, :], x[FULL * P:N, :]).then_inc(s_x, 16)
                        n = 2
                    sp.wait_ge(s_wz, 1)
                    for q in range(NQ):
                        rows = wl[q * D:(q + 1) * D]
                        sp.dma_start(rows[:, 0:KA, :], w_bond.rearrange("k (i j) -> i k j", j=D)).then_inc(s_w, 16)
                        sp.dma_start(rows[:, KA, :], b_bond.rearrange("(i j) -> i j", j=D)).then_inc(s_w, 16)
                    sp.dma_start(wg[0:D], w_ih.rearrange("(b g) j -> g b j", g=D)).then_inc(s_w, 16)
                    sp.dma_start(wg[D:2 * D], w_hh.rearrange("(b g) j -> g b j", g=D)).then_inc(s_w, 16)
                    sp.dma_start(wx[2 * D:2 * D + 1, 0:3 * D], b_ih.rearrange("(a g) -> a g", a=1)).then_inc(s_w, 16)
                    sp.dma_start(wx[2 * D + 1:2 * D + 2, 0:2 * D], b_hh[0:2 * D].rearrange("(a g) -> a g", a=1)).then_inc(s_w, 16)
                    sp.dma_start(wx[2 * D + 1:2 * D + 2, 3 * D:4 * D], b_hh[2 * D:3 * D].rearrange("(a g) -> a g", a=1)).then_inc(s_w, 16)
                    sp.wait_ge(s_xz, 2)
                    sp.dma_start(node_rows(ht, HG * P), cat[:, :, D:2 * D]).then_inc(s_h0, 16)
                    sp.wait_ge(s_h0, 16)

                @block.scalar
                def _(act):
                    act.wait_ge(s_sq, 1)
                    act.sqrt(var[:], var[:]).then_inc(s_sqd, 1)

                @block.vector
                def _(dve):
                    ch = Chain(dve, s_cv, steps_v[0])
                    ch(dve.memset(xs[:, FULL:HG, :], 0.0)) if FULL < HG else None
                    dve.sem_inc(s_xz, 1)
                    ch(dve.memset(wx[:], 0.0))
                    dve.sem_inc(s_wz, 1)
                    ch(dve.memset(wb[:], 0.0))
                    ch(dve.memset(cat[:], 1.0))
                    ch(dve.tensor_copy(pni[:], part_f[:]))
                    ch(dve.tensor_scalar(pni[:], pni[:], QP - 1, CH.bit_length() - 1, ALU.bitwise_and, ALU.logical_shift_right))
                    ch(dve.tensor_copy(pn[:], pni[:]))
                    ch(dve.tensor_scalar(mask4[:], iota1_f[:, 0:CPT], -1.0, pn[:, 0:1], ALU.add, ALU.is_equal))
                    dve.wait_ge(s_x, 16 * (2 if REST else 1))
                    norm_relu(dve, ch, xs[:], cat[:, :, D:2 * D], tmp[:])
                    dve.sem_inc(s_xz, 1)
                    dve.wait_ge(s_w, 16 * (2 * NQ + 5))
                    ch(dve.transpose(wlt[:].rearrange("p k j -> p (k j)"), wl[:].rearrange("p k j -> p (k j)")))
                    for q in range(NQ):
                        a = q * D
                        ch(dve.tensor_copy(wb[a:a + D, :, a:a + D], wlt[a:a + D]))
                    ch(dve.transpose(wgt[:].rearrange("p k j -> p (k j)"), wg[:].rearrange("p k j -> p (k j)")))
                    ch(dve.tensor_copy(wx[0:D, 0:3 * D], wgt[0:D].rearrange("p k j -> p (k j)")))
                    ch(dve.tensor_copy(wx[D:2 * D, 0:2 * D], wgt[D:2 * D, 0:2].rearrange("p k j -> p (k j)")))
                    ch(dve.tensor_copy(wx[D:2 * D, 3 * D:4 * D], wgt[D:2 * D, 2]))
                    steps_v[0] += ch.n

            s_m = sem("flags_loaded")
            s_rec = [sem(f"rec3_loaded{b}") for b in range(2)]
            s_hg = [[sem(f"h_gathered{b}_{half}") for half in range(2)] for b in range(2)]
            s_a = sem("a_made")
            s_t = sem("outer_in_psum")
            s_tdone = sem("outer_products_done")
            s_ts = sem("outer_copied")
            s_msg = sem("messages")
            s_scan = sem("scanned")
            s_tr = sem("scan_transposed")
            s_sc = sem("scan_copied")
            s_st = [sem(f"scan_stored{b}") for b in range(2)]
            s_cr = sem("carries_loaded")
            s_g = [sem(f"sums_gathered{g}") for g in range(NG)]
            s_agg = sem("aggregated")
            s_catt = sem("cat_transposed")
            s_ct = sem("cat_t_copied")
            s_gate = sem("gates_in_psum")
            s_sig = sem("sigmoid_done")
            s_pre = sem("pre_tanh")
            s_tanh = sem("tanh_done")
            s_new = sem("h_new")
            s_hw = sem("h_stored")
            s_v6 = sem("step_chain")
            rows3 = r3.rearrange("(i p u) w -> i p (u w)", p=P, u=J3)
            st_rows = st.rearrange("(q i c) d -> i c q d", q=NQ, c=NT)
            GPB = 512 // (4 * K1 * CPT) * 4
            GPB = 4
            NB = J3 // GPB
            RING = 4
            with ExitStack() as c7:
                sb, pb = alloc(c7)
                carry_m = sb("carry_mask", [P, QC])
                rec = [sb(f"rec3_{b}", [P, J3, W3]) for b in range(2)]
                hb = [sb(f"h_rows{b}", [P, J3, D]) for b in range(2)]
                am = [sb(f"a_masked{b}", [P, J3, K1, CPT]) for b in range(2)]
                ts = [sb(f"outer_sums{b}", [P, K1, J3 * CPT]) for b in range(2)]
                sc = [sb(f"scan{b}", [P, NT]) for b in range(2)]
                sct = [sb(f"scan_t{b}", [P, P]) for b in range(2)]
                sums = sb("sums", [P, HG, D])
                cr = sb("carries", [P, NQ - 1, D])
                crt = sb("carry_tmp", [P, GB, D])
                ct = sb("cat_t", [2 * D + 2, GB, P])
                rz = sb("rz", [P, GB, 2 * D])
                tn = sb("tn", [P, GB, D])
                tw = sb("tw", [P, GB, D])
                pt = [pb(f"outer{k}", [P, 512]) for k in range(RING)]
                pm = pb("msg_psum", [P, 512])
                px = pb("scan_t_psum", [P, 512])
                pg = pb("gates", [P, 8, P])
                block = c7.enter_context(nc.Block())

                def nsteps(eng, body):
                    with eng.Fori(0, STEPS) as s:
                        body(s)

                @block.sync
                def _(sp):
                    for q in range(NQ):
                        sp.dma_start(carry_m[q * QP:(q + 1) * QP, :],
                                     flags[q * QC:(q + 1) * QC, :].rearrange("c w -> w c").broadcast_to([QP, QC])).then_inc(s_m, 16)

                    def step(s):
                        def load(it, b, i):
                            sp.wait_ge(s_tdone, s * IT3 + it + 1)
                            sp.dma_start(rec[b][:], rows3[bass.ds(it, 1)].rearrange("a p w -> (a p) w")).then_inc(s_rec[b], 16)
                        pairs(sp, IT3, load)
                        for b in range(2):
                            sp.wait_ge(s_st[b], s * (8 * IT3) + 8 * IT3)
                        for q in range(NQ - 1):
                            sp.dma_start(cr[:, q, :], st[QC * (q + 1) - 1:QC * (q + 1), :].broadcast_to([P, D])).then_inc(s_cr, 16)
                        for g in range(NG):
                            sp.wait_ge(s_new, s * NG + g + 1)
                            sp.dma_start(ht[g * GB * P:(g + 1) * GB * P].rearrange("(h l) d -> l h d", l=P),
                                         cat[:, g * GB:(g + 1) * GB, D:2 * D]).then_inc(s_hw, 16)
                        sp.wait_ge(s_hw, s * (16 * NG) + 16 * NG)
                        hold(sp)
                    nsteps(sp, step)

                @block.gpsimd
                def _(pool):
                    def step(s):
                        pool.wait_ge(s_hw, s * (16 * NG))
                        hold(pool)

                        def gather(it, b, i):
                            pool.wait_ge(s_rec[b], s * (8 * IT3) + i * 16 + 16)
                            pool.wait_ge(s_tdone, s * IT3 + it + 1)
                            hold(pool)
                            for u in range(J3):
                                pool.indirect_dma_start(
                                    out=hb[b][:, u, :], out_offset=None, in_=ht,
                                    in_offset=bass.IndirectOffsetOnAxis(ap=rec[b][:, u, W_DST:W_DST + 1].bitcast(I32), axis=0)
                                ).then_inc(s_hg[b][u // (J3 // 2)], 16)
                        pairs(pool, IT3, gather)
                        for b in range(2):
                            pool.wait_ge(s_st[b], s * (8 * IT3) + 8 * IT3)
                        hold(pool)
                        for g in range(NG):
                            for h in range(g * GB, (g + 1) * GB):
                                pool.indirect_dma_start(
                                    out=sums[:, h, :], out_offset=None, in_=st,
                                    in_offset=bass.IndirectOffsetOnAxis(ap=last_chunk[:, h:h + 1], axis=0)).then_inc(s_g[g], 16)
                    nsteps(pool, step)

                @block.vector
                def _(dve):
                    K = 2 * (NQ - 1) * NG + 3 * NG
                    dve.wait_ge(s_m, 16 * NQ)
                    dve.memset(sc[1][:], 0.0).then_inc(s_v6, 1)
                    dve.wait_ge(s_v6, 1)

                    def step(s):
                        def body(it, b, i):
                            dve.wait_ge(s_rec[b], s * (8 * IT3) + i * 16 + 16)
                            dve.wait_ge(s_tdone, s * IT3 + it + 1)
                            dve.tensor_tensor(am[b][:], rec[b][:, :, 0:K1].unsqueeze(3).broadcast_to([P, J3, K1, CPT]),
                                              mask4[:].unsqueeze(1).unsqueeze(1).broadcast_to([P, J3, K1, CPT]),
                                              ALU.mult).then_inc(s_a, 1)
                            dve.wait_ge(s_msg, s * IT3 + it + 3)
                            dve.wait_ge(s_scan, s * IT3 + it)
                            dve.wait_ge(s_tr, s * IT3 + it + 1)
                            dve.tensor_tensor_scan(sc[b][:], carry_m[:, bass.ds(it * NT, NT)], pm[:, 0:NT],
                                                   sc[1 - b][:, NT - 1:NT], ALU.mult, ALU.add).then_inc(s_scan, 1)
                        pairs(dve, IT3, body)
                        dve.wait_ge(s_tr, s * IT3 + IT3 + 2)
                        dve.memset(sc[1][:, NT - 1:NT], 0.0).then_inc(s_v6, 1)
                        dve.wait_ge(s_cr, s * (16 * (NQ - 1)) + 16 * (NQ - 1))
                        ch = Chain(dve, s_v6, s * (K + 1) + 2)
                        dve.wait_ge(s_v6, s * (K + 1) + 2)

                        def aggregate(g):
                            c = slice(g * GB, (g + 1) * GB)
                            dve.wait_ge(s_g[g], s * (16 * GB) + 16 * GB)
                            agg = cat[:, c, 0:D]
                            ch(dve.tensor_tensor(agg, sums[:, c, :], has_edges[:, c].unsqueeze(2).broadcast_to([P, GB, D]), ALU.mult))
                            for q in range(NQ - 1):
                                ch(dve.tensor_tensor(crt[:], cr[:, q, :].unsqueeze(1).broadcast_to([P, GB, D]),
                                                     spans[:, q, c].unsqueeze(2).broadcast_to([P, GB, D]), ALU.mult))
                                add = dve.tensor_tensor(agg, agg, crt[:], ALU.add)
                                if q < NQ - 2:
                                    ch(add)
                                else:
                                    add.then_inc(s_agg, 1)
                                    dve.wait_ge(s_agg, s * NG + g + 1)

                        def update(g):
                            c = slice(g * GB, (g + 1) * GB)
                            h = cat[:, c, D:2 * D]
                            dve.wait_ge(s_sig, s * NG + g + 1)
                            ch(dve.tensor_tensor(tn[:], rz[:, :, 0:D], pg[:, 0:GB, 3 * D:4 * D], ALU.mult))
                            dve.tensor_tensor(tn[:], tn[:], pg[:, 0:GB, 2 * D:3 * D], ALU.add).then_inc(s_pre, 1)
                            dve.wait_ge(s_tanh, s * NG + g + 1)
                            ch(dve.tensor_tensor(tw[:], h, tn[:], ALU.subtract))
                            ch(dve.tensor_tensor(tw[:], tw[:], rz[:, :, D:2 * D], ALU.mult))
                            dve.tensor_tensor(h, tw[:], tn[:], ALU.add).then_inc(s_new, 1)
                            dve.wait_ge(s_new, s * NG + g + 1)
                        aggregate(0)
                        for g in range(NG):
                            if g + 1 < NG:
                                aggregate(g + 1)
                            update(g)
                        assert ch.n == (2 * (NQ - 1)) * NG + 3 * NG == K, (ch.n, K)
                    nsteps(dve, step)

                @block.tensor
                def _(pe):
                    pe.sem_inc(s_tdone, 2)
                    pe.sem_inc(s_msg, 2)
                    pe.sem_inc(s_tr, 2)

                    def step(s):
                        def body(it, b, i):
                            n = s * IT3 + it
                            pe.wait_ge(s_a, n + 1)
                            for g in range(NB):
                                if g % (NB // 2) == 0:
                                    pe.wait_ge(s_hg[b][g // (NB // 2)], s * (4 * J3 * IT3) + i * (8 * J3) + 8 * J3)
                                pe.wait_ge(s_ts, n * NB + g + 1)
                                hold(pe)
                                for u in range(g * GPB, (g + 1) * GPB):
                                    for q in range(NQ):
                                        k = slice(q * QP, (q + 1) * QP)
                                        at = (u - g * GPB) * K1 * CPT
                                        last = pe.matmul(pt[g % RING][k, at:at + K1 * CPT], hb[b][k, u, :], am[b][k, u, :, :],
                                                         start=True, stop=True, tile_position=(q * QP, q * QP))
                                last.then_inc(s_t, 1)
                            pe.wait_ge(s_t, n * NB + NB)
                            pe.sem_inc(s_tdone, 1)
                            pe.wait_ge(s_ts, n * NB + NB + RING)
                            pe.wait_ge(s_scan, n)
                            for k in range(K1):
                                last = pe.matmul(pm[:, 0:NT], wb[:, k, :], ts[b][:, k, :], start=(k == 0), stop=(k == K1 - 1))
                            last.then_inc(s_msg, 1)
                            pe.wait_ge(s_scan, n + 1)
                            pe.wait_ge(s_sc, n)
                            pe.transpose(px[:, 0:P], sc[b][:], ident_f[:]).then_inc(s_tr, 1)
                        pairs(pe, IT3, body)
                        for g in range(NG):
                            pe.wait_ge(s_agg, s * NG + g + 1)
                            pe.wait_ge(s_ct, s * NG + g)
                            for h in range(GB):
                                last = pe.transpose(pt[h // 4][0:2 * D + 2, (h % 4) * P:(h % 4 + 1) * P],
                                                    cat[:, g * GB + h, :], ident_f[:])
                            last.then_inc(s_catt, 1)
                            pe.wait_ge(s_ct, s * NG + g + 1)
                            pe.wait_ge(s_pre, s * NG + g)
                            for h in range(GB):
                                last = pe.matmul(pg[:, h, :], ct[:, h, :], wx[:], start=True, stop=True)
                            last.then_inc(s_gate, 1)
                    nsteps(pe, step)

                @block.scalar
                def _(act):
                    act.sem_inc(s_ts, RING)

                    def step(s):
                        def body(it, b, i):
                            n = s * IT3 + it
                            act.wait_ge(s_msg, n + 1)
                            for g in range(NB):
                                act.wait_ge(s_t, n * NB + g + 1)
                                w = GPB * CPT
                                act.copy(ts[b][:, :, g * w:(g + 1) * w].rearrange("p k (u c) -> p u k c", c=CPT),
                                         pt[g % RING][:, 0:GPB * K1 * CPT].rearrange("p (u k c) -> p u k c", u=GPB, k=K1)
                                         ).then_inc(s_ts, 1)
                            act.wait_ge(s_tr, n + 3)
                            act.wait_ge(s_st[b], s * (8 * IT3) + i * 16)
                            act.copy(sct[b][:], px[:, 0:P]).then_inc(s_sc, 1)
                            act.wait_ge(s_sc, n + 1)
                            act.dma_start(st_rows[bass.ds(it, 1)].rearrange("a c q d -> (a c) q d"),
                                          sct[b][:].rearrange("c (q d) -> c q d", d=D)).then_inc(s_st[b], 16)
                        pairs(act, IT3, body)
                        for g in range(NG):
                            act.wait_ge(s_catt, s * NG + g + 1)
                            act.wait_ge(s_gate, s * NG + g)
                            act.copy(ct[:, 0:4, :], pt[0][0:2 * D + 2, :].rearrange("p (h l) -> p h l", l=P))
                            act.copy(ct[:, 4:GB, :], pt[1][0:2 * D + 2, 0:(GB - 4) * P].rearrange("p (h l) -> p h l", l=P)).then_inc(s_ct, 1)
                            act.wait_ge(s_gate, s * NG + g + 1)
                            act.wait_ge(s_new, s * NG + g)
                            act.activation(rz[:], pg[:, 0:GB, 0:2 * D], ACT.Sigmoid).then_inc(s_sig, 1)
                            act.wait_ge(s_pre, s * NG + g + 1)
                            act.activation(tn[:], tn[:], ACT.Tanh).then_inc(s_tanh, 1)
                    nsteps(act, step)

            s_ldm = [sem(f"r2_for_messages{b}") for b in range(2)]
            s_om = sem("onehots_m")
            s_tm = sem("onehots_m_transposed")
            s_otm = sem("onehots_m_copied")
            s_xm = sem("picked")
            s_xg = sem("groups_picked")
            s_mm = sem("messages_made")
            s_ms = [sem(f"messages_scattered{b}") for b in range(2)]
            s_g7 = sem("g_made")
            s_v7 = sem("message_chain")
            with ExitStack() as c8:
                sb, pb = alloc(c8)
                tmp = sb("ln_tmp2", [P, HG, D])
                deg = sb("deg", [P, HG])
                rec = [sb(f"rec7_{b}", [P, J2, W2]) for b in range(2)]
                om = [sb(f"om{b}", [P, J2, P], BF16) for b in range(2)]
                otm = [sb(f"otm{b}", [P, 4, P]) for b in range(2)]
                ms = [sb(f"ms{b}", [P, J2, D + 1]) for b in range(2)]
                fx = sb("fx", [P, J2])
                ix = [sb(f"ix{b}", [P, J2], I32) for b in range(2)]
                ptm = [pb(f"ptm{b}", [P, 8, P], BF16) for b in range(2)]
                pxm = [pb(f"pxm{b}", [P, J2, D]) for b in range(2)]
                block = c8.enter_context(nc.Block())
                G = J2 // 4

                @block.sync
                def _(sp):
                    def load(it, b, i):
                        sp.wait_ge(s_mm, it + 1)
                        sp.dma_start(rec[b][:], tiles2[bass.ds(it, 1)].rearrange("a p w -> (a p) w")).then_inc(s_ldm[b], 16)
                    pairs(sp, IT2, load)

                @block.vector
                def _(dve):
                    ch = Chain(dve, s_cv, steps_v[0])
                    ch(dve.tensor_tensor(xs[:], xs[:], cat[:, :, D:2 * D], ALU.add))
                    norm_relu(dve, ch, xs[:], gt[:], tmp[:])
                    ch(dve.memset(dis[:], 0.0))
                    ch(dve.memset(deg[:], 1.0))
                    ch(dve.tensor_scalar(deg[:, 0:HB], node_d[:, 0:HB], 1.0, None, ALU.max))
                    ch(dve.tensor_copy(var[:], deg[:]))
                    dve.sem_inc(s_sq, 1)
                    s_ln[0] += 1
                    dve.wait_ge(s_sqd, s_ln[0])
                    ch(dve.reciprocal(deg[:], var[:]))
                    ch(dve.tensor_scalar(dis[:, 0:HB], node_d[:, 0:HB], 0.5, None, ALU.is_gt))
                    ch(dve.tensor_tensor(dis[:], dis[:], deg[:], ALU.mult))
                    ch(dve.tensor_tensor(gt[:], gt[:], dis[:].unsqueeze(2).broadcast_to([P, HG, D]), ALU.mult))
                    steps_v[0] += ch.n
                    dve.sem_inc(s_g7, 1)
                    dve.sem_inc(s_mm, 2)

                    def body(it, b, i):
                        dve.wait_ge(s_ldm[b], i * 16 + 16)
                        dve.wait_ge(s_xm, it + 1)
                        for u in range(J2):
                            o = dve.tensor_scalar(om[b][:, u, :], iota1_b[:], rec[b][:, u, W_LO_S:W_LO_S + 1], None, ALU.is_equal)
                            if u % 4 == 3:
                                o.then_inc(s_om, 1)
                        dve.wait_ge(s_ms[b], i * (16 * J2))
                        dve.tensor_scalar(fx[:], rec[b][:, :, W_ONE], -float(BIG), float(BIG), ALU.mult, ALU.add).then_inc(s_v7, 1)
                        dve.tensor_copy(ix[b][:], rec[b][:, :, W_POS_D].bitcast(I32)).then_inc(s_v7, 1)
                        dve.tensor_copy(ms[b][:, :, D], rec[b][:, :, W_LO_D])
                        dve.wait_ge(s_v7, it * 3 + 2)
                        dve.tensor_tensor(ix[b][:], ix[b][:], fx[:], ALU.add).then_inc(s_v7, 1)
                        dve.wait_ge(s_v7, it * 3 + 3)
                        dve.wait_ge(s_xm, it + 3)
                        dve.tensor_tensor(ms[b][:, :, 0:D], pxm[b][:],
                                          rec[b][:, :, W_WEIGHT:W_WEIGHT + 1].broadcast_to([P, J2, D]), ALU.mult).then_inc(s_mm, 1)
                    pairs(dve, IT2, body)

                @block.scalar
                def _(act):
                    for n in (2, 3):
                        act.wait_ge(s_sq, n)
                        act.sqrt(var[:], var[:]).then_inc(s_sqd, 1)
                    act.sem_inc(s_otm, 2)

                    def body(it, b, i):
                        for g in range(G):
                            act.wait_ge(s_tm, it * G + g + 1)
                            act.wait_ge(s_xg, it * G + g + 1)
                            act.copy(otm[g % 2][:], ptm[g % 2][:, 0:4, :]).then_inc(s_otm, 1)
                    pairs(act, IT2, body)

                @block.tensor
                def _(pe):
                    pe.sem_inc(s_xm, 2)
                    pe.sem_inc(s_xg, 2)
                    pe.wait_ge(s_g7, 1)

                    def pick(it, b, g, h):
                        pe.wait_ge(s_otm, it * G + g + 3)
                        for k in range(4):
                            last = pe.matmul(pxm[b][:, 4 * g + k, :], otm[g % 2][:, k, :],
                                             gt[:].rearrange("p h d -> p (h d)")[:, bass.ds(h[k] * D, D)], start=True, stop=True)
                        last.then_inc(s_xg, 1)

                    def body(it, b, i):
                        pe.wait_ge(s_mm, it + 1)
                        for g in range(G):
                            pe.wait_ge(s_om, it * G + g + 1)
                            pe.wait_ge(s_otm, it * G + g + 1)
                            for k in range(4):
                                last = pe.transpose(ptm[g % 2][:, k, :], om[b][:, 4 * g + k, :], ident_b[:])
                            last.then_inc(s_tm, 1)
                            h = hi_registers(pe, pack_s, it * G + g)
                            pick(it, b, g, h)
                        pe.wait_ge(s_xg, it * G + G + 2)
                        pe.sem_inc(s_xm, 1)
                    pairs(pe, IT2, body)

                @block.gpsimd
                def _(pool):
                    def scatter(it, b, i):
                        pool.wait_ge(s_mm, it + 3)
                        hold(pool)
                        for u in range(J2):
                            pool.indirect_dma_start(
                                out=m2, out_offset=bass.IndirectOffsetOnAxis(ap=ix[b][:, u:u + 1], axis=0),
                                in_=ms[b][:, u, :], in_offset=None,
                                bounds_check=T2 * P - 1, oob_is_err=False).then_inc(s_ms[b], 16)
                    pairs(pool, IT2, scatter)
                    for b in range(2):
                        pool.wait_ge(s_ms[b], 16 * J2 * (IT2 // 2))

            s_ldn = [sem(f"messages_loaded{b}") for b in range(2)]
            s_on = sem("onehots_n")
            s_sum = sem("messages_summed")
            s_acc0 = sem("sums_cleared")
            s_z8 = sem("zeros_8")
            s_y = sem("y_made")
            s_out = sem("out_stored")
            rows8 = m2.rearrange("(i p u) w -> i p (u w)", p=P, u=J2)
            with ExitStack() as c9:
                sb, pb = alloc(c9)
                mr = [sb(f"mr{b}", [P, J2, D + 1]) for b in range(2)]
                on = [sb(f"on{b}", [P, J2, P]) for b in range(2)]
                zero = sb("zero8", [P, 512])
                y = sb("y", [P, HB, D])
                acc = pb("node_sums", [P, 7 * 512])
                block = c9.enter_context(nc.Block())
                G = J2 // 4

                @block.sync
                def _(sp):
                    def load(it, b, i):
                        sp.wait_ge(s_sum, it + 1)
                        sp.dma_start(mr[b][:], rows8[bass.ds(it, 1)].rearrange("a p w -> (a p) w")).then_inc(s_ldn[b], 16)
                    pairs(sp, IT2, load)
                    sp.wait_ge(s_y, 1)
                    n = 0
                    if FULL:
                        sp.dma_start(node_rows(out, FULL * P), y[:, 0:FULL, :]).then_inc(s_out, 16)
                        n += 16
                    if REST:
                        sp.dma_start(out[FULL * P:N, :], y[0:REST, FULL, :]).then_inc(s_out, 16)
                        n += 16
                    sp.wait_ge(s_out, n)

                @block.vector
                def _(dve):
                    dve.memset(zero[:], 0.0).then_inc(s_z8, 1)

                    def build(it, b, i):
                        dve.wait_ge(s_ldn[b], i * 16 + 16)
                        dve.wait_ge(s_sum, it + 1)
                        for u in range(J2):
                            last = dve.tensor_scalar(on[b][:, u, :], iota1_f[:], mr[b][:, u, D:D + 1], None, ALU.is_equal)
                        last.then_inc(s_on, 1)
                    pairs(dve, IT2, build)
                    dve.wait_ge(s_sum, IT2 + 2)
                    ch = Chain(dve, s_cv, steps_v[0])
                    ch(dve.tensor_tensor(y[:], acc[:, 0:HB * D].rearrange("p (h d) -> p h d", d=D),
                                         dis[:, 0:HB].unsqueeze(2).broadcast_to([P, HB, D]), ALU.mult))
                    dve.tensor_tensor(y[:], y[:], xs[:, 0:HB, :], ALU.add).then_inc(s_y, 1)

                @block.tensor
                def _(pe):
                    pe.sem_inc(s_sum, 2)
                    pe.wait_ge(s_z8, 1)
                    for k in range(7):
                        pe.matmul(acc[:, 512 * k:512 * k + 512], zero[:, 0:P], zero[:], start=True, stop=False, skip_group_check=True)

                    def body(it, b, i):
                        regs = [hi_registers(pe, pack_d, it * G + g) for g in range(G)]
                        pe.wait_ge(s_on, it + 1)
                        for u in range(J2):
                            last = pe.matmul(acc[:, bass.ds(regs[u // 4][u % 4] * D, D)], on[b][:, u, :], mr[b][:, u, 0:D],
                                             start=False, stop=False, skip_group_check=True)
                        last.then_inc(s_sum, 1)
                    pairs(pe, IT2, body)


_INS = ["x", "src", "dst", "edge_attr_16", "edge_weight", "L0_gnn_W_bond", "L0_gnn_b_bond", "L0_gnn_W_ih",
        "L0_gnn_W_hh", "L0_gnn_b_ih", "L0_gnn_b_hh"]


def kernel(**inputs):
    import numpy as _np
    import concourse.bacc as _bacc
    from concourse import mybir as _mybir
    from concourse.bass_utils import run_bass_kernel_spmd as _run

    nc = _bacc.Bacc("TRN2", target_bir_lowering=False, num_devices=1)
    arrays, args = {}, []
    for name in _INS:
        a = _np.ascontiguousarray(inputs[name])
        arrays[f"in_{name}_dram"] = a
        args.append(nc.dram_tensor(f"in_{name}_dram", a.shape, _mybir.dt.from_np(a.dtype), kind="ExternalInput").ap())
    shape = inputs["x"].shape
    args.append(nc.dram_tensor("out_0_dram", shape, _mybir.dt.float32, kind="ExternalOutput").ap())
    gnn_program(nc, *args)
    r = _run(nc, [arrays], core_ids=[0])
    return r.results[0]["out_0_dram"]
```

```python
from contextlib import ExitStack

import concourse.bass as bass
from concourse import mybir

F32 = mybir.dt.float32
BF16 = mybir.dt.bfloat16
I32 = mybir.dt.int32
ALU = mybir.AluOpType
ACT = mybir.ActivationFunctionType
AX = mybir.AxisListType

P = 128
STEPS = 4
CH = 4
NQ = 4
QP = P // NQ
CPT = QP // CH
J1 = 25
J2 = 16
J3 = P // CPT
GB = 7
BIG = 1 << 23
EPS = 1e-5

W_ONE, W_DST, W_WEIGHT, W_POS_D, W_LO_D, W3 = 16, 17, 18, 19, 20, 21
K1 = 17


def up(a, b):
    return -(-a // b) * b


class Chain:

    def __init__(self, engine, sem, base=0):
        self.engine, self.sem, self.base, self.n = engine, sem, base, 0

    def __call__(self, instruction):
        instruction.then_inc(self.sem, 1)
        self.n += 1
        self.engine.wait_ge(self.sem, self.base + self.n)


def pairs(engine, total, body):
    with engine.Fori(0, total // 2) as i:
        body(i * 2, 0, i)
        body(i * 2 + 1, 1, i)
    if total % 2:
        body(total - 1, 0, total // 2)


def pairs_after_first(engine, total, body):
    body(0, 0, 0, True)
    if total > 2:
        with engine.Fori(0, (total - 1) // 2) as i:
            body(i * 2 + 1, 1, i, False)
            body(i * 2 + 2, 0, i + 1, False)
    if total % 2 == 0:
        body(total - 1, 1, total // 2 - 1, False)


def gnn_program(nc, x, src, dst, attr, weight, w_bond, b_bond, w_ih, w_hh, b_ih, b_hh, out):
    N, D = x.shape
    E = src.shape[0]
    KA = attr.shape[1]
    assert D == 32 and KA == 16 and E % (P * J1) == 0
    HB = up(N, P) // P
    HG = up(HB, GB)
    NG = HG // GB
    T1 = E // P
    IT1 = T1 // J1
    T2 = up(T1 + HB, 2 * J2)
    IT2 = T2 // J2
    T3 = up(-(-(E + N * (CH - 1)) // P), 2 * J3)
    IT3 = T3 // J3
    QS = T3 * QP
    QC = QS // CH
    NCH = NQ * QC
    FULL = N // P
    REST = N - FULL * P
    NT = J3 * CPT
    assert T3 * P < BIG and T2 * P < BIG and HB <= P and HB * D <= 7 * 512 and NT == P and T2 % 4 == 0

    r3 = nc.dram_tensor("edges_by_node", [T3 * P, W3], F32).ap()
    m2 = nc.dram_tensor("messages_by_bucket", [T2 * P, D + 1], F32).ap()
    st = nc.dram_tensor("chunk_sums", [NCH, D], F32).ap()
    ht = nc.dram_tensor("h_table", [HG * P, D], F32).ap()
    gx = nc.dram_tensor("g_by_chunk", [NCH, D], F32).ap()
    flags = nc.dram_tensor("carry_flags", [NCH, 1], F32).ap()

    outer = ExitStack()
    with outer:
        def sem(name):
            return outer.enter_context(nc.semaphore(name))

        def alloc(stack):
            def sb(name, shape, dt=F32):
                return stack.enter_context(nc.sbuf_tensor(name, shape, dt))

            def pb(name, shape, dt=F32):
                return stack.enter_context(nc.psum_tensor(name, shape, dt))
            return sb, pb

        sb, _ = alloc(outer)
        iota_b = sb("iota_b", [P, P], BF16)
        iota1_f = sb("iota1_f", [P, P])
        part_f = sb("part_f", [P, 1])
        ident_f = sb("ident_f", [P, P])
        ident_b = sb("ident_b", [P, P], BF16)
        after_b = sb("after_b", [P, P], BF16)
        rest_b = sb("rest_b", [P, P], BF16)
        before_f = sb("before_f", [P, P])
        before_b = sb("before_b", [P, P], BF16)
        ones_f = sb("ones_f", [P, P])
        zrow = sb("zrow", [P, 1])
        pack_d = sb("pack_d", [1, T2 // 4], I32)
        node_s = sb("node_s", [P, P])
        node_d = sb("node_d", [P, P])
        last_chunk = sb("last_chunk", [P, HG], I32)
        has_edges = sb("has_edges", [P, HG])
        spans = sb("spans_quarter_end", [P, NQ - 1, HG])
        flag_at = sb("flag_at", [P, HB], I32)
        s_cv = sem("vector_chain")
        steps_v = [0]

        s_seen = sem("waits_seen")

        def hold(engine):
            engine.sem_inc(s_seen, 1)

        def hi_registers(eng, pack, word):
            w = eng.value_load(pack[0:1, bass.ds(word, 1)], min_val=0, max_val=(1 << 28) - 1)
            return [nc.s_assert_within((w // (1 << (7 * k))) % 128, 0, HB - 1,
                                       skip_runtime_bounds_check_because="buckets are numbered below HB")
                    for k in range(4)]

        with ExitStack() as sort:
            sb, pb = alloc(sort)
            lo_s = sb("lo_s", [P, IT1 + 1, J1], BF16)
            hi_s = sb("hi_s", [P, IT1 + 1, J1], BF16)
            lo_d = sb("lo_d", [P, IT1 + 1, J1], BF16)
            hi_d = sb("hi_d", [P, IT1 + 1, J1], BF16)

            def onehots(eng, out, key, width):
                n = out.shape[1]
                return eng.tensor_tensor(out, iota_b[:, 0:width].unsqueeze(1).broadcast_to([P, n, width]),
                                         key.unsqueeze(2).broadcast_to([P, n, width]), ALU.is_equal)

            def of(keys, it):
                return keys[:, bass.ds(it, 1), :].rearrange("p a u -> p (a u)")

            s_keys = sem("keys_loaded")
            s_iota = sem("iotas_made")
            s_const = sem("constants_made")
            s_split = sem("keys_split")
            s_zero = sem("zeros_made")
            s_fill = sem("tables_cleared")
            s_oh_v = sem("onehots_by_vector")
            s_oh_a = sem("onehots_by_scalar")
            s_neg = sem("keys_negated")
            s_dist = sem("distances_made")
            s_cnt = sem("edges_counted")
            with ExitStack() as c1:
                sb, pb = alloc(c1)
                oh_s = [sb(f"oh_s{b}", [P, J1, P], BF16) for b in range(2)]
                oh_hs = [sb(f"oh_hs{b}", [P, J1, HB], BF16) for b in range(2)]
                oh_hd = [sb(f"oh_hd{b}", [P, J1, HB], BF16) for b in range(2)]
                oh_d = [sb(f"oh_d{b}", [P, J1, P], BF16) for b in range(2)]
                dist = sb("distance", [P, J1, P], BF16)
                key_v = [sb(f"key_v{b}", [P, 3, J1], BF16) for b in range(2)]
                neg = [sb(f"neg_lo_d{b}", [P, J1]) for b in range(2)]
                key_i = sb("key_i", [P, IT1, J1], I32)
                tmp_i = sb("tmp_i", [P, IT1, J1], I32)
                zeros = sb("zeros", [P, 3200])
                one_fill = sb("one_fill", [P, NCH // P])
                iota_f = sb("iota_f", [P, P])
                iota_i = sb("iota_i", [P, P], I32)
                part_i = sb("part_i", [P, 1], I32)
                pnode_s = pb("pnode_s", [P, P])
                pnode_d = pb("pnode_d", [P, P])
                block = c1.enter_context(nc.Block())

                @block.sync
                def _(sp):
                    sp.dma_start(key_i[:], src.rearrange("(i p u) -> p i u", p=P, u=J1)).then_inc(s_keys, 16)
                    sp.wait_ge(s_split, 1)
                    sp.dma_start(key_i[:], dst.rearrange("(i p u) -> p i u", p=P, u=J1)).then_inc(s_keys, 16)
                    sp.wait_ge(s_zero, 1)
                    n = 0
                    for table in (r3, m2, gx):
                        flat = table.rearrange("(p a) w -> p (a w)", p=P)
                        for at in range(0, flat.shape[1], 3200):
                            m = min(3200, flat.shape[1] - at)
                            sp.dma_start(flat[:, at:at + m], zeros[:, 0:m]).then_inc(s_fill, 16)
                            n += 1
                    sp.dma_start(flags.rearrange("(p a) w -> p (a w)", p=P), one_fill[:]).then_inc(s_fill, 16)
                    sp.wait_ge(s_fill, 16 * (n + 1))

                @block.gpsimd
                def _(pool):
                    pool.iota(iota_i[:], [[1, P]], base=0, channel_multiplier=0).then_inc(s_iota, 1)
                    pool.iota(part_i[:], [[1, 1]], base=0, channel_multiplier=1).then_inc(s_iota, 1)
                    pool.memset(zeros[:], 0.0).then_inc(s_iota, 1)
                    pool.memset(one_fill[:], 1.0).then_inc(s_iota, 1)
                    pool.wait_ge(s_iota, 4)
                    pool.sem_inc(s_zero, 1)

                @block.vector
                def _(dve):
                    ch = Chain(dve, s_cv, steps_v[0])
                    dve.wait_ge(s_iota, 2)
                    ch(dve.tensor_copy(iota_f[:], iota_i[:]))
                    ch(dve.tensor_copy(iota_b[:], iota_i[:]))
                    ch(dve.tensor_copy(part_f[:], part_i[:]))
                    ch(dve.tensor_scalar(iota1_f[:], iota_f[:], 1.0, None, ALU.add))
                    ch(dve.tensor_scalar(ident_f[:], iota_f[:], part_f[:, 0:1], None, ALU.is_equal))
                    ch(dve.tensor_copy(ident_b[:], ident_f[:]))
                    ch(dve.tensor_scalar(before_f[:], iota_f[:], part_f[:, 0:1], None, ALU.is_gt))
                    ch(dve.tensor_copy(before_b[:], before_f[:]))
                    ch(dve.tensor_scalar(after_b[:], iota_f[:], part_f[:, 0:1], None, ALU.is_lt))
                    ch(dve.tensor_scalar(rest_b[:], iota_f[:], part_f[:, 0:1], None, ALU.is_le))
                    ch(dve.memset(ones_f[:], 1.0))
                    ch(dve.memset(zrow[:], 0.0))
                    ch(dve.memset(oh_s[1][:, 0, :], 0.0))
                    dve.sem_inc(s_const, 1)
                    for keys in (lo_s, hi_s, lo_d, hi_d):
                        ch(dve.memset(keys[:, IT1], 0.0))
                    for n, (hi, lo) in enumerate(((hi_s, lo_s), (hi_d, lo_d))):
                        dve.wait_ge(s_keys, 16 * (n + 1))
                        ch(dve.tensor_scalar(tmp_i[:], key_i[:], 7, None, ALU.logical_shift_right))
                        ch(dve.tensor_copy(hi[:, 0:IT1], tmp_i[:]))
                        ch(dve.tensor_scalar(tmp_i[:], key_i[:], 127, None, ALU.bitwise_and))
                        ch(dve.tensor_copy(lo[:, 0:IT1], tmp_i[:]))
                        dve.sem_inc(s_split, 1)
                    base = steps_v[0] + ch.n

                    def build(it, b, i):
                        dve.wait_ge(s_cnt, it + 1)
                        st_ = Chain(dve, s_cv, it * 3 + base)
                        for k, key in enumerate((lo_s, hi_s, hi_d)):
                            st_(dve.tensor_copy(key_v[b][:, k, :], of(key, it)))
                        onehots(dve, oh_s[b][:], key_v[b][:, 0, :], P)
                        onehots(dve, oh_hs[b][:], key_v[b][:, 1, :], HB)
                        onehots(dve, oh_hd[b][:], key_v[b][:, 2, :], HB).then_inc(s_oh_v, 1)
                    pairs(dve, IT1, build)
                    ch.n += 3 * IT1
                    dve.wait_ge(s_cnt, IT1 + 2)
                    ch(dve.tensor_copy(node_s[:, 0:HB], pnode_s[:, 0:HB]))
                    ch(dve.tensor_copy(node_d[:, 0:HB], pnode_d[:, 0:HB]))
                    steps_v[0] += ch.n

                @block.scalar
                def _(act):
                    act.wait_ge(s_split, 2)

                    def build(it, b, i):
                        act.wait_ge(s_cnt, it + 1)
                        act.mul(neg[b][:], of(lo_d, it), -1.0).then_inc(s_neg, 1)
                        act.wait_ge(s_neg, it + 1)
                        act.wait_ge(s_oh_a, it)
                        for u in range(J1):
                            last = act.activation(dist[:, u, :], iota_b[:], ACT.Abs, bias=neg[b][:, u:u + 1], scale=1.0)
                        last.then_inc(s_dist, 1)
                        act.wait_ge(s_dist, it + 1)
                        act.activation(oh_d[b][:], dist[:], ACT.Relu, bias=ones_f[:, 0:1], scale=-1.0).then_inc(s_oh_a, 1)
                    pairs(act, IT1, build)

                @block.tensor
                def _(pe):
                    pe.wait_ge(s_const, 1)
                    for acc in (pnode_s, pnode_d):
                        clear = pe.matmul(acc[:], oh_s[1][:, 0, :], ident_b[:], start=True, stop=False, skip_group_check=True)
                    clear.then_inc(s_cnt, 2)

                    def count(it, b, i):
                        pe.wait_ge(s_oh_v, it + 1)
                        pe.wait_ge(s_oh_a, it + 1)
                        for u in range(J1):
                            pe.matmul(pnode_s[:, 0:HB], oh_s[b][:, u, :], oh_hs[b][:, u, :], start=False, stop=False, skip_group_check=True)
                            last = pe.matmul(pnode_d[:, 0:HB], oh_d[b][:, u, :], oh_hd[b][:, u, :], start=False, stop=False, skip_group_check=True)
                        last.then_inc(s_cnt, 1)
                    pairs(pe, IT1, count)

            sb, _ = alloc(sort)
            slots = sb("first_slot", [P, HB])
            starts = sb("bucket_start", [P, HB])
            s_io2 = sem("tile_numbers")
            s_pv = sem("sums_wanted")
            s_pp = sem("sums_in_psum")
            with ExitStack() as c2:
                sb, pb = alloc(c2)
                tile_i = sb("tile_i", [P, T2], I32)
                tile_f = sb("tile_f", [P, T2])
                at_or_after = sb("at_or_after", [P, T2])
                hi_t = sb("bucket_of_tile", [P, T2])
                tb = sb("bucket_tile", [P, 1])
                ni = sb("ni", [P, HB], I32)
                nchunk = sb("nchunk", [P, HB])
                first = sb("first_chunk", [P, HB])
                colsum = sb("colsum", [P, HB])
                t1 = sb("plan_tmp", [P, HB])
                ps = pb("plan_psum", [P, 512])
                block = c2.enter_context(nc.Block())
                spans_of = [(a, min(512, T2 - a)) for a in range(0, T2, 512)]
                asked = [0]
                jobs = []

                @block.gpsimd
                def _(pool):
                    pool.iota(tile_i[:], [[1, T2]], base=0, channel_multiplier=0).then_inc(s_io2, 1)

                @block.vector
                def _(dve):
                    ch = Chain(dve, s_cv, steps_v[0])
                    one = ones_f[:, 0:1].broadcast_to([P, HB])

                    def product(*job):
                        jobs.append(job)
                        dve.sem_inc(s_pv, 1)
                        asked[0] += 1
                        dve.wait_ge(s_pp, asked[0])

                    product(ps[:, 0:HB], ones_f[:], node_d[:, 0:HB])
                    ch(dve.tensor_scalar(ni[:], ps[:, 0:HB], float(P - 1), None, ALU.add))
                    ch(dve.tensor_scalar(ni[:], ni[:], 7, None, ALU.logical_shift_right))
                    ch(dve.tensor_copy(t1[:], ni[:]))
                    ch(dve.tensor_tensor_scan(starts[:], one, t1[:], 0.0, ALU.mult, ALU.add))
                    ch(dve.tensor_tensor(starts[:], starts[:], t1[:], ALU.subtract))
                    product("transpose", ps[0:HB, 0:P], starts[:])
                    ch(dve.tensor_copy(tb[0:HB, :], ps[0:HB, 0:1]))
                    ch(dve.tensor_scalar(starts[:], starts[:], float(P), None, ALU.mult))
                    dve.wait_ge(s_io2, 1)
                    ch(dve.tensor_copy(tile_f[:], tile_i[:]))
                    ch(dve.tensor_scalar(at_or_after[0:HB], tile_f[0:HB], tb[0:HB, 0:1], None, ALU.is_ge))
                    for a, m in spans_of:
                        product(ps[:, 0:m], ones_f[0:HB, :], at_or_after[0:HB, a:a + m])
                        ch(dve.tensor_scalar(hi_t[:, a:a + m], ps[:, 0:m], -1.0, None, ALU.add))
                    ch(dve.tensor_copy(tile_i[0:1, :], hi_t[0:1, :]))
                    four = tile_i[0:1, :].rearrange("p (w k) -> p w k", k=4)
                    for j in (1, 2, 3):
                        ch(dve.tensor_scalar(four[:, :, j], four[:, :, j], 7 * j, None, ALU.logical_shift_left))
                        ch(dve.tensor_tensor(four[:, :, 0], four[:, :, 0], four[:, :, j], ALU.bitwise_or))
                    ch(dve.tensor_copy(pack_d[:].bitcast(F32), four[:, :, 0].bitcast(F32)))
                    nd = node_s[:, 0:HB]
                    ch(dve.tensor_scalar(ni[:], nd, float(CH - 1), None, ALU.add))
                    ch(dve.tensor_scalar(ni[:], ni[:], CH.bit_length() - 1, None, ALU.logical_shift_right))
                    ch(dve.tensor_copy(nchunk[:], ni[:]))
                    product(ps[:, 0:HB], ones_f[:], nchunk[:])
                    ch(dve.tensor_copy(colsum[:], ps[:, 0:HB]))
                    ch(dve.tensor_tensor_scan(first[:], one, colsum[:], 0.0, ALU.mult, ALU.add))
                    ch(dve.tensor_tensor(first[:], first[:], colsum[:], ALU.subtract))
                    product(ps[:, 0:HB], before_f[:], nchunk[:])
                    ch(dve.tensor_tensor(first[:], first[:], ps[:, 0:HB], ALU.add))
                    ch(dve.tensor_scalar(slots[:], first[:], float(CH), None, ALU.mult))
                    ch(dve.memset(has_edges[:], 0.0))
                    ch(dve.memset(last_chunk[:], 0))
                    ch(dve.memset(spans[:], 0.0))
                    ch(dve.tensor_scalar(has_edges[:, 0:HB], nd, 0.5, None, ALU.is_gt))
                    ch(dve.tensor_tensor(t1[:], first[:], nchunk[:], ALU.add))
                    ch(dve.tensor_scalar(t1[:], t1[:], -1.0, 0.0, ALU.add, ALU.max))
                    ch(dve.tensor_copy(last_chunk[:, 0:HB], t1[:]))
                    for q in range(NQ - 1):
                        sp_ = spans[:, q, 0:HB]
                        ch(dve.scalar_tensor_tensor(out=sp_, in0=t1[:], scalar=float(QC * (q + 1)), in1=has_edges[:, 0:HB],
                                                    op0=ALU.is_ge, op1=ALU.mult))
                        ch(dve.scalar_tensor_tensor(out=sp_, in0=first[:], scalar=float(QC * (q + 1)), in1=sp_,
                                                    op0=ALU.is_lt, op1=ALU.mult))
                    ch(dve.tensor_scalar(t1[:], has_edges[:, 0:HB], -float(BIG), float(BIG), ALU.mult, ALU.add))
                    ch(dve.tensor_tensor(t1[:], t1[:], first[:], ALU.add))
                    ch(dve.tensor_copy(flag_at[:], t1[:]))
                    steps_v[0] += ch.n

                @block.tensor
                def _(pe):
                    for n, job in enumerate(jobs):
                        pe.wait_ge(s_pv, n + 1)
                        if job[0] == "transpose":
                            pe.transpose(job[1], job[2], ident_f[:]).then_inc(s_pp, 1)
                        else:
                            pe.matmul(job[0], job[1], job[2], start=True, stop=True).then_inc(s_pp, 1)

            s_ld = [sem(f"edges_loaded{b}") for b in range(2)]
            s_row = sem("rows_made")
            s_sc = [sem(f"rows_scattered{b}") for b in range(2)]
            s_v3 = sem("place_chain")
            s_flag = sem("flags_scattered")
            s_init = sem("starts_in_psum")
            s_ob = sem("onehots_built")
            s_obd = sem("dst_onehots_built")
            s_nd = sem("dst_keys_negated")
            s_dd = sem("dst_distances_made")
            s_kv = sem("keys_copied")
            s_tp = sem("onehots_transposed")
            s_ev = sem("transposes_copied")
            s_same = sem("src_row_in_psum")
            s_nf = sem("next_free_copied")
            s_look = sem("slots_looked_up")
            s_add = sem("tile_added")
            s_bx = sem("earlier_of_bucket")
            s_bxr = sem("bucket_place_read")
            s_lr = sem("slot_read")
            s_rp = sem("repetitions_counted")
            s_place = sem("places_made")
            with ExitStack() as c3:
                sb, pb = alloc(c3)
                at_ = [sb(f"attr{b}", [P, J1, KA]) for b in range(2)]
                wt = [sb(f"weight{b}", [P, J1]) for b in range(2)]
                di = [sb(f"dst{b}", [P, J1], I32) for b in range(2)]
                row = [sb(f"row{b}", [P, J1, W3]) for b in range(2)]
                key_v = [sb(f"key3_{b}", [P, 2, J1], BF16) for b in range(2)]
                key_f = [sb(f"key3_f{b}", [P, 3, J1]) for b in range(2)]
                key_t = [sb(f"key_t{b}", [2 * J1, P], BF16) for b in range(2)]
                row_of = sb("row_of", [2 * J1, J1, P], BF16)
                negd = [sb(f"neg_hi_d{b}", [P, J1]) for b in range(2)]
                distd = [sb(f"distance3_{b}", [P, HB], BF16) for b in range(2)]
                o_lo = [sb(f"o_lo{b}", [P, J1, P], BF16) for b in range(2)]
                o_hi = [sb(f"o_hi{b}", [P, J1, HB], BF16) for b in range(2)]
                o_bd = [sb(f"o_bd{b}", [P, J1, HB], BF16) for b in range(2)]
                ot_f = [sb(f"ot_f{b}", [P, P]) for b in range(2)]
                nfs = [sb(f"next_free{b}", [P, HB]) for b in range(2)]
                junk = sb("junk", [P, HB])
                rep_ = [sb(f"repetitions{b}", [P, J1]) for b in range(2)]
                look = [sb(f"looked_up{b}", [P, J1]) for b in range(2)]
                bpos = [sb(f"bucket_place{b}", [P, J1]) for b in range(2)]
                place = [sb(f"place{b}", [P, J1], I32) for b in range(2)]
                slot = sb("slot", [P, J1])
                quarter = sb("quarter", [P, J1])
                si = sb("slot_i", [P, J1], I32)
                ti = sb("slot_t", [P, J1], I32)
                ptp = [pb(f"ptp{b}", [P, 8, P], BF16) for b in range(2)]
                psame = [pb(f"psame{b}", [P, 512]) for b in range(2)]
                plook = [pb(f"plook{b}", [P, 512]) for b in range(2)]
                nextf = pb("nextf", [P, 512])
                nextb = pb("nextb", [P, 512])
                block = c3.enter_context(nc.Block())
                LS = QP.bit_length() - 1
                L3 = J3.bit_length() - 1
                L2 = J2.bit_length() - 1

                def ring(b, u):
                    return (b * J1 + u) % 2

                @block.sync
                def _(sp):
                    def load(it, b, i):
                        sp.wait_ge(s_row, it + 1)
                        e = bass.ds(it * (P * J1), P * J1)
                        sp.dma_start(at_[b][:], attr[e, :].rearrange("(p u) k -> p u k", p=P)).then_inc(s_ld[b], 16)
                        sp.dma_start(wt[b][:], weight[e].rearrange("(p u) -> p u", p=P)).then_inc(s_ld[b], 16)
                        sp.dma_start(di[b][:], dst[e].rearrange("(p u) -> p u", p=P)).then_inc(s_ld[b], 16)
                    pairs(sp, IT1, load)

                @block.tensor
                def _(pe):
                    pe.matmul(nextf[:, 0:HB], ident_f[:], slots[:], start=True, stop=False, skip_group_check=True)
                    pe.matmul(nextb[:, 0:HB], ident_f[:], starts[:], start=True, stop=False, skip_group_check=True).then_inc(s_init, 1)

                    def body(it, b, i):
                        def turn(u):
                            k = ring(b, u)
                            if u <= 1:
                                pe.wait_ge(s_ob, it * J1 + u + 1)
                            if u == 0:
                                hold(pe)
                                pe.transpose(ptp[k][0:2 * J1, 1, :], key_v[b][:].rearrange("p a u -> p (a u)"), ident_b[:])
                            pe.transpose(ptp[k][:, 0, :], o_lo[b][:, u, :], ident_b[:]).then_inc(s_tp, 1)

                        def rest(u):
                            pe.wait_ge(s_bxr, it * J1 + u + 1)
                            pe.matmul(nextb[:, 0:HB], rest_b[:], o_bd[b][:, u, :], start=False, stop=False, skip_group_check=True)
                        turn(0)
                        for u in range(J1):
                            t, k = it * J1 + u, ring(b, u)
                            if u:
                                rest(u - 1)
                            if u == 0:
                                pe.wait_ge(s_obd, t + 1)
                            pe.matmul(nextb[:, 0:HB], before_b[:], o_bd[b][:, u, :], start=False, stop=False,
                                      skip_group_check=True).then_inc(s_bx, 1)
                            if u + 1 < J1:
                                turn(u + 1)
                            pe.wait_ge(s_ev, t + 3)
                            pe.matmul(psame[k][:, 0:P], row_of[:, u, :], key_t[b][:], start=True, stop=True).then_inc(s_same, 1)
                            pe.wait_ge(s_nf, t + 1)
                            pe.matmul(nextf[:, 0:HB], o_lo[b][:, u, :], o_hi[b][:, u, :], start=False, stop=False,
                                      skip_group_check=True).then_inc(s_add, 1)
                            pe.matmul(plook[k][:, 0:HB], ot_f[k][:], nfs[k][:], start=True, stop=True).then_inc(s_look, 1)
                        rest(J1 - 1)
                    pe.sem_inc(s_look, 2)
                    pairs(pe, IT1, body)

                @block.scalar
                def _(act):
                    act.sem_inc(s_row, 2)
                    act.sem_inc(s_ev, 2)
                    act.wait_ge(s_init, 1)

                    def negate(it, b):
                        act.mul(negd[b][:], of(hi_d, it), -1.0).then_inc(s_nd, 1)

                    def build_bd(it, b, u):
                        t, k = it * J1 + u, ring(b, u)
                        if u == 0:
                            act.wait_ge(s_nd, it + 1)
                        act.activation(distd[k][:], iota_b[:, 0:HB], ACT.Abs, bias=negd[b][:, u:u + 1], scale=1.0).then_inc(s_dd, 1)
                        act.wait_ge(s_dd, t + 1)
                        act.activation(o_bd[b][:, u, :], distd[k][:], ACT.Relu, bias=ones_f[:, 0:1], scale=-1.0).then_inc(s_obd, 1)
                    negate(0, 0)
                    build_bd(0, 0, 0)
                    build_bd(0, 0, 1)

                    def body(it, b, i):
                        def copy(u):
                            t, k = it * J1 + u, ring(b, u)
                            act.wait_ge(s_tp, t + 1)
                            if u == 0:
                                act.copy(key_t[b][:], ptp[k][0:2 * J1, 1, :])
                            act.copy(ot_f[k][:], ptp[k][:, 0, :]).then_inc(s_ev, 1)
                        copy(0)
                        for u in range(J1):
                            t, k = it * J1 + u, ring(b, u)
                            act.wait_ge(s_add, t)
                            act.copy(nfs[k][:], nextf[:, 0:HB]).then_inc(s_nf, 1)
                            if u + 1 < J1:
                                copy(u + 1)
                            if u == J1 - 3:
                                negate(it + 1, 1 - b)
                            if u + 2 < J1:
                                build_bd(it, b, u + 2)
                            else:
                                build_bd(it + 1, 1 - b, u + 2 - J1)
                        act.wait_ge(s_ld[b], i * 48 + 48)
                        act.wait_ge(s_sc[b], i * (16 * J1))
                        act.copy(row[b][:, :, 0:KA], at_[b][:])
                        act.copy(row[b][:, :, W_WEIGHT], wt[b][:])
                        act.copy(row[b][:, :, W_DST].bitcast(I32), di[b][:])
                        act.add(row[b][:, :, W_LO_D], of(lo_d, it), 1.0).then_inc(s_row, 1)
                    pairs(act, IT1, body)

                @block.vector
                def _(dve):
                    KP = 18
                    AHEAD = 3
                    c0 = Chain(dve, s_v3)
                    c0(dve.memset(row[0][:, :, W_ONE], 1.0))
                    c0(dve.memset(row[1][:, :, W_ONE], 1.0))
                    for u in range(J1):
                        c0(dve.tensor_scalar(row_of[:, u, :], part_f[0:2 * J1, 0:1].broadcast_to([2 * J1, P]), float(u), float(P),
                                             ALU.is_equal, ALU.mult))
                        c0(dve.scalar_tensor_tensor(out=row_of[:, u, :], in0=part_f[0:2 * J1, 0:1].broadcast_to([2 * J1, P]),
                                                    scalar=float(u + J1), in1=row_of[:, u, :], op0=ALU.is_equal, op1=ALU.add))
                    base = c0.n
                    dve.sem_inc(s_lr, 2)
                    dve.sem_inc(s_rp, 2)
                    dve.sem_inc(s_place, 2)
                    dve.wait_ge(s_init, 1)

                    def take_keys(it, b):
                        for n, key in enumerate((hi_s, lo_s)):
                            dve.tensor_copy(key_v[b][:, n, :], of(key, it)).then_inc(s_kv, 1)
                        for n, key in enumerate((lo_s, hi_s)):
                            dve.tensor_copy(key_f[b][:, n, :], of(key, it)).then_inc(s_kv, 1)
                        dve.wait_ge(s_kv, it * 5 + 4)
                        dve.scalar_tensor_tensor(out=key_f[b][:, 2, :], in0=key_f[b][:, 1, :], scalar=float(P), in1=key_f[b][:, 0, :],
                                                 op0=ALU.mult, op1=ALU.add).then_inc(s_kv, 1)
                        dve.wait_ge(s_kv, it * 5 + 5)

                    def build(it, b, u):
                        dve.tensor_scalar(o_lo[b][:, u, :], iota_b[:], key_f[b][:, 0, u:u + 1], None, ALU.is_equal)
                        dve.tensor_scalar(o_hi[b][:, u, 0:HB], iota_b[:, 0:HB], key_f[b][:, 1, u:u + 1], None, ALU.is_equal).then_inc(s_ob, 1)

                    def place_r3_a(ch, b):
                        ch(dve.tensor_tensor(slot[:], look[b][:], rep_[b][:], ALU.add))
                        ch(dve.tensor_scalar(quarter[:], slot[:], float(QS), None, ALU.is_ge))
                        for q in (2, 3):
                            ch(dve.scalar_tensor_tensor(out=quarter[:], in0=slot[:], scalar=float(q * QS), in1=quarter[:],
                                                        op0=ALU.is_ge, op1=ALU.add))
                        ch(dve.scalar_tensor_tensor(out=si[:], in0=quarter[:], scalar=-float(QS), in1=slot[:],
                                                    op0=ALU.mult, op1=ALU.add))

                    def place_r3_b(ch, b):
                        ch(dve.tensor_scalar(ti[:], si[:], LS, J3 - 1, ALU.logical_shift_right, ALU.bitwise_and))
                        ch(dve.tensor_copy(slot[:], ti[:]))
                        ch(dve.scalar_tensor_tensor(out=quarter[:], in0=quarter[:], scalar=float(QP * J3), in1=slot[:],
                                                    op0=ALU.mult, op1=ALU.add))

                    def place_r3_c(ch, b):
                        ch(dve.tensor_scalar(ti[:], si[:], QP - 1, L3, ALU.bitwise_and, ALU.logical_shift_left))
                        ch(dve.tensor_scalar(si[:], si[:], LS + L3, 7 + L3, ALU.logical_shift_right, ALU.logical_shift_left))
                        ch(dve.tensor_tensor(si[:], si[:], ti[:], ALU.bitwise_or))
                        ch(dve.tensor_copy(slot[:], si[:]))
                        ch(dve.tensor_tensor(place[b][:], slot[:], quarter[:], ALU.add))

                    def place_m2_a(ch, b):
                        ch(dve.tensor_copy(si[:], bpos[b][:]))
                        ch(dve.tensor_scalar(ti[:], si[:], 7, J2 - 1, ALU.logical_shift_right, ALU.bitwise_and))

                    def place_m2_b(ch, b):
                        pos = row[b][:, :, W_POS_D].bitcast(I32)
                        ch(dve.tensor_scalar(pos, si[:], P - 1, L2, ALU.bitwise_and, ALU.logical_shift_left))
                        ch(dve.tensor_tensor(ti[:], ti[:], pos, ALU.bitwise_or))
                        ch(dve.tensor_scalar(si[:], si[:], 7 + L2, 7 + L2, ALU.logical_shift_right, ALU.logical_shift_left))
                        dve.tensor_tensor(pos, si[:], ti[:], ALU.bitwise_or).then_inc(s_place, 1)

                    stages = (place_r3_a, place_r3_b, place_r3_c, place_m2_a, place_m2_b)

                    def place_stage(n, ch, it, b, i):
                        if n == 0:
                            dve.wait_ge(s_lr, it * J1 + J1 + 2)
                            dve.wait_ge(s_bxr, it * J1 + J1)
                            dve.wait_ge(s_rp, it * J1 + J1 + 2)
                            dve.wait_ge(s_sc[b], i * (16 * J1))
                            dve.wait_ge(s_place, it + 2)
                        stages[n](ch, b)
                    take_keys(0, 0)
                    for u in range(AHEAD):
                        build(0, 0, u)

                    def body(it, b, i, first):
                        ch = Chain(dve, s_v3, (it - 1) * KP + base) if not first else None
                        for u in range(J1):
                            t, k = it * J1 + u, ring(b, u)
                            dve.wait_ge(s_bx, t + 1)
                            dve.tensor_tensor_reduce(out=junk[:], in0=nextb[:, 0:HB], in1=o_bd[b][:, u, :], scale=1.0, scalar=0.0,
                                                     op0=ALU.mult, op1=ALU.add, accum_out=bpos[b][:, u:u + 1]).then_inc(s_bxr, 1)
                            dve.wait_ge(s_same, t + 1)
                            dve.scalar_tensor_tensor(out=psame[k][:, 0:P], in0=psame[k][:, 0:P], scalar=key_f[b][:, 2, u:u + 1],
                                                     in1=after_b[:], op0=ALU.is_equal, op1=ALU.mult,
                                                     accum_out=rep_[b][:, u:u + 1]).then_inc(s_rp, 1)
                            if u == J1 - AHEAD - 1:
                                take_keys(it + 1, 1 - b)
                            if u + AHEAD < J1:
                                build(it, b, u + AHEAD)
                            else:
                                build(it + 1, 1 - b, u + AHEAD - J1)
                            dve.wait_ge(s_look, t + 3)
                            dve.tensor_tensor_reduce(out=plook[k][:, 0:HB], in0=plook[k][:, 0:HB], in1=o_hi[b][:, u, :],
                                                     scale=1.0, scalar=0.0, op0=ALU.mult, op1=ALU.add,
                                                     accum_out=look[b][:, u:u + 1]).then_inc(s_lr, 1)
                            if not first and u % 4 == 2 and u // 4 < len(stages):
                                place_stage(u // 4, ch, it - 1, 1 - b, i + b - 1)
                        assert first or ch.n == KP, ch.n
                    pairs_after_first(dve, IT1, body)
                    last = IT1 - 1
                    ch = Chain(dve, s_v3, last * KP + base)
                    for n in range(len(stages)):
                        place_stage(n, ch, last, last % 2, last // 2)

                @block.gpsimd
                def _(pool):
                    for h in range(HB):
                        pool.indirect_dma_start(
                            out=flags, out_offset=bass.IndirectOffsetOnAxis(ap=flag_at[:, h:h + 1], axis=0),
                            in_=zrow[:], in_offset=None, bounds_check=NCH - 1, oob_is_err=False).then_inc(s_flag, 16)

                    def scatter(it, b, i):
                        pool.wait_ge(s_row, it + 3)
                        pool.wait_ge(s_place, it + 3)
                        hold(pool)
                        for u in range(J1):
                            pool.indirect_dma_start(
                                out=r3, out_offset=bass.IndirectOffsetOnAxis(ap=place[b][:, u:u + 1], axis=0),
                                in_=row[b][:, u, :], in_offset=None).then_inc(s_sc[b], 16)
                    pairs(pool, IT1, scatter)
                    pool.wait_ge(s_sc[0], 16 * J1 * ((IT1 + 1) // 2))
                    pool.wait_ge(s_sc[1], 16 * J1 * (IT1 // 2))
                    pool.wait_ge(s_flag, 16 * HB)

        lay = ExitStack()
        with lay:
            sb, _ = alloc(lay)
            xs = sb("x_nodes", [P, HG, D])
            cat = sb("agg_h_one", [P, HG, 2 * D + 2])
            wb = sb("w_bond_blocks", [P, K1, P])
            wx = sb("w_gru", [2 * D + 2, 4 * D])
            mask4 = sb("chunk_of_row", [P, CPT])
            sums = sb("sums_then_g", [P, HG, D])
            carry_m = sb("carry_mask", [P, QC], BF16)
            mean = sb("mean", [P, HG])
            var = sb("var", [P, HG])
            dis = sb("deg_inv_sqrt", [P, HG])
            s_x = sem("x_loaded")
            s_xz = sem("x_cleared")
            s_w = sem("weights_loaded")
            s_wz = sem("weights_cleared")
            s_sq = sem("sqrt_wanted")
            s_sqd = sem("sqrt_done")
            s_h0 = sem("h0_stored")
            s_m = [sem(f"flags_loaded{b}") for b in range(2)]
            s_mc = sem("flags_copied")

            s_ln = [0]

            def norm_relu(dve, ch, xin, xout, tmp):
                ch(dve.tensor_reduce(mean[:], xin, AX.X, ALU.add))
                ch(dve.tensor_scalar(mean[:], mean[:], 1.0 / D, None, ALU.mult))
                ch(dve.tensor_tensor(tmp, xin, mean[:].unsqueeze(2).broadcast_to([P, HG, D]), ALU.subtract))
                ch(dve.tensor_tensor(xout, tmp, tmp, ALU.mult))
                ch(dve.tensor_reduce(var[:], xout, AX.X, ALU.add))
                ch(dve.tensor_scalar(var[:], var[:], 1.0 / D, EPS, ALU.mult, ALU.add))
                dve.sem_inc(s_sq, 1)
                s_ln[0] += 1
                dve.wait_ge(s_sqd, s_ln[0])
                ch(dve.reciprocal(mean[:], var[:]))
                ch(dve.tensor_tensor(tmp, tmp, mean[:].unsqueeze(2).broadcast_to([P, HG, D]), ALU.mult))
                ch(dve.tensor_scalar(xout, tmp, 0.0, None, ALU.max))

            def node_rows(table, rows):
                return table[0:rows].rearrange("(h l) d -> l h d", l=P)

            with ExitStack() as c6:
                sb, pb = alloc(c6)
                wl = sb("w_bond_rows", [P, K1, D])
                wlt = sb("w_bond_cols", [P, K1, D])
                wg = sb("w_gru_rows", [2 * D, 3, D])
                wgt = sb("w_gru_cols", [2 * D, 3, D])
                tmp = sb("ln_tmp", [P, HG, D])
                pn = sb("pn", [P, 1])
                pni = sb("pni", [P, 1], I32)
                stage = [sb(f"flag_stage{b}", [P, 2048]) for b in range(2)]
                parts = [(a, min(2048, QC - a)) for a in range(0, QC, 2048)]
                block = c6.enter_context(nc.Block())

                @block.sync
                def _(sp):
                    sp.wait_ge(s_xz, 1)
                    n = 1
                    sp.dma_start(xs[:, 0:FULL, :], node_rows(x, FULL * P)).then_inc(s_x, 16)
                    if REST:
                        sp.dma_start(xs[0:REST, FULL, :], x[FULL * P:N, :]).then_inc(s_x, 16)
                        n = 2
                    sp.wait_ge(s_wz, 1)
                    for q in range(NQ):
                        rows = wl[q * D:(q + 1) * D]
                        sp.dma_start(rows[:, 0:KA, :], w_bond.rearrange("k (i j) -> i k j", j=D)).then_inc(s_w, 16)
                        sp.dma_start(rows[:, KA, :], b_bond.rearrange("(i j) -> i j", j=D)).then_inc(s_w, 16)
                    sp.dma_start(wg[0:D], w_ih.rearrange("(b g) j -> g b j", g=D)).then_inc(s_w, 16)
                    sp.dma_start(wg[D:2 * D], w_hh.rearrange("(b g) j -> g b j", g=D)).then_inc(s_w, 16)
                    sp.dma_start(wx[2 * D:2 * D + 1, 0:3 * D], b_ih.rearrange("(a g) -> a g", a=1)).then_inc(s_w, 16)
                    sp.dma_start(wx[2 * D + 1:2 * D + 2, 0:2 * D], b_hh[0:2 * D].rearrange("(a g) -> a g", a=1)).then_inc(s_w, 16)
                    sp.dma_start(wx[2 * D + 1:2 * D + 2, 3 * D:4 * D], b_hh[2 * D:3 * D].rearrange("(a g) -> a g", a=1)).then_inc(s_w, 16)
                    for n, (at, m) in enumerate(parts):
                        if n >= 2:
                            sp.wait_ge(s_mc, n - 1)
                        for q in range(NQ):
                            rows = flags[q * QC + at:q * QC + at + m, :]
                            sp.dma_start(stage[n % 2][q * QP:(q + 1) * QP, 0:m],
                                         rows.rearrange("c w -> w c").broadcast_to([QP, m])).then_inc(s_m[n % 2], 16)
                    sp.wait_ge(s_xz, 2)
                    sp.dma_start(node_rows(ht, HG * P), cat[:, :, D:2 * D]).then_inc(s_h0, 16)
                    sp.wait_ge(s_h0, 16)

                @block.scalar
                def _(act):
                    act.wait_ge(s_sq, 1)
                    act.sqrt(var[:], var[:]).then_inc(s_sqd, 1)
                    for n, (at, m) in enumerate(parts):
                        act.wait_ge(s_m[n % 2], 16 * NQ * (n // 2 + 1))
                        act.copy(carry_m[:, at:at + m], stage[n % 2][:, 0:m]).then_inc(s_mc, 1)

                @block.vector
                def _(dve):
                    ch = Chain(dve, s_cv, steps_v[0])
                    ch(dve.memset(xs[:, FULL:HG, :], 0.0)) if FULL < HG else None
                    dve.sem_inc(s_xz, 1)
                    ch(dve.memset(wx[:], 0.0))
                    dve.sem_inc(s_wz, 1)
                    ch(dve.memset(wb[:], 0.0))
                    ch(dve.memset(cat[:], 1.0))
                    ch(dve.tensor_copy(pni[:], part_f[:]))
                    ch(dve.tensor_scalar(pni[:], pni[:], QP - 1, CH.bit_length() - 1, ALU.bitwise_and, ALU.logical_shift_right))
                    ch(dve.tensor_copy(pn[:], pni[:]))
                    ch(dve.tensor_scalar(mask4[:], iota1_f[:, 0:CPT], -1.0, pn[:, 0:1], ALU.add, ALU.is_equal))
                    dve.wait_ge(s_x, 16 * (2 if REST else 1))
                    norm_relu(dve, ch, xs[:], cat[:, :, D:2 * D], tmp[:])
                    dve.sem_inc(s_xz, 1)
                    dve.wait_ge(s_w, 16 * (2 * NQ + 5))
                    ch(dve.transpose(wlt[:].rearrange("p k j -> p (k j)"), wl[:].rearrange("p k j -> p (k j)")))
                    for q in range(NQ):
                        a = q * D
                        ch(dve.tensor_copy(wb[a:a + D, :, a:a + D], wlt[a:a + D]))
                    ch(dve.transpose(wgt[:].rearrange("p k j -> p (k j)"), wg[:].rearrange("p k j -> p (k j)")))
                    ch(dve.tensor_copy(wx[0:D, 0:3 * D], wgt[0:D].rearrange("p k j -> p (k j)")))
                    ch(dve.tensor_copy(wx[D:2 * D, 0:2 * D], wgt[D:2 * D, 0:2].rearrange("p k j -> p (k j)")))
                    ch(dve.tensor_copy(wx[D:2 * D, 3 * D:4 * D], wgt[D:2 * D, 2]))
                    steps_v[0] += ch.n

            s_rec = [sem(f"rec3_loaded{b}") for b in range(2)]
            s_hg = [[sem(f"h_gathered{b}_{half}") for half in range(2)] for b in range(2)]
            s_a = sem("a_made")
            s_t = sem("outer_in_psum")
            s_tdone = sem("outer_products_done")
            s_ts = sem("outer_copied")
            s_msg = sem("messages")
            s_scan = sem("scanned")
            s_tr = sem("scan_transposed")
            s_sc = sem("scan_copied")
            s_st = [sem(f"scan_stored{b}") for b in range(2)]
            s_cr = sem("carries_loaded")
            s_g = [sem(f"sums_gathered{g}") for g in range(NG)]
            s_agg = sem("aggregated")
            s_catt = sem("cat_transposed")
            s_ct = sem("cat_t_copied")
            s_gate = sem("gates_in_psum")
            s_sig = sem("sigmoid_done")
            s_pre = sem("pre_tanh")
            s_tanh = sem("tanh_done")
            s_new = sem("h_new")
            s_hw = sem("h_stored")
            s_v6 = sem("step_chain")
            rows3 = r3.rearrange("(i p u) w -> i p (u w)", p=P, u=J3)
            st_rows = st.rearrange("(q i c) d -> i c q d", q=NQ, c=NT)
            GPB = 16 // CPT
            NB = J3 // GPB
            RING = 4
            with ExitStack() as c7:
                sb, pb = alloc(c7)
                rec = [sb(f"rec3_{b}", [P, J3, W3]) for b in range(2)]
                hb = [sb(f"h_rows{b}", [P, J3, D]) for b in range(2)]
                am = [sb(f"a_masked{b}", [P, J3, K1, CPT]) for b in range(2)]
                ts = [sb(f"outer_sums{b}", [P, K1, J3 * CPT]) for b in range(2)]
                sc = [sb(f"scan{b}", [P, NT]) for b in range(2)]
                sct = [sb(f"scan_t{b}", [P, P]) for b in range(2)]
                cr = sb("carries", [P, NQ - 1, D])
                crt = sb("carry_tmp", [P, GB, D])
                ct = sb("cat_t", [2 * D + 2, GB, P])
                rz = sb("rz", [P, GB, 2 * D])
                tn = sb("tn", [P, GB, D])
                tw = sb("tw", [P, GB, D])
                pt = [pb(f"outer{k}", [P, 512]) for k in range(RING)]
                pm = pb("msg_psum", [P, 512])
                px = pb("scan_t_psum", [P, 512])
                pg = pb("gates", [P, 8, P])
                block = c7.enter_context(nc.Block())

                def nsteps(eng, body):
                    with eng.Fori(0, STEPS) as s:
                        body(s)

                @block.sync
                def _(sp):
                    def step(s):
                        def load(it, b, i):
                            sp.wait_ge(s_tdone, s * IT3 + it + 1)
                            sp.dma_start(rec[b][:], rows3[bass.ds(it, 1)].rearrange("a p w -> (a p) w")).then_inc(s_rec[b], 16)
                        pairs(sp, IT3, load)
                        for b in range(2):
                            sp.wait_ge(s_st[b], s * (8 * IT3) + 8 * IT3)
                        for q in range(NQ - 1):
                            sp.dma_start(cr[:, q, :], st[QC * (q + 1) - 1:QC * (q + 1), :].broadcast_to([P, D])).then_inc(s_cr, 16)
                        for g in range(NG):
                            sp.wait_ge(s_new, s * NG + g + 1)
                            sp.dma_start(ht[g * GB * P:(g + 1) * GB * P].rearrange("(h l) d -> l h d", l=P),
                                         cat[:, g * GB:(g + 1) * GB, D:2 * D]).then_inc(s_hw, 16)
                        sp.wait_ge(s_hw, s * (16 * NG) + 16 * NG)
                        hold(sp)
                    nsteps(sp, step)

                @block.gpsimd
                def _(pool):
                    def step(s):
                        pool.wait_ge(s_hw, s * (16 * NG))
                        hold(pool)

                        def gather(it, b, i):
                            pool.wait_ge(s_rec[b], s * (8 * IT3) + i * 16 + 16)
                            pool.wait_ge(s_tdone, s * IT3 + it + 1)
                            hold(pool)
                            for u in range(J3):
                                pool.indirect_dma_start(
                                    out=hb[b][:, u, :], out_offset=None, in_=ht,
                                    in_offset=bass.IndirectOffsetOnAxis(ap=rec[b][:, u, W_DST:W_DST + 1].bitcast(I32), axis=0)
                                ).then_inc(s_hg[b][u // (J3 // 2)], 16)
                        pairs(pool, IT3, gather)
                        for b in range(2):
                            pool.wait_ge(s_st[b], s * (8 * IT3) + 8 * IT3)
                        hold(pool)
                        for g in range(NG):
                            for h in range(g * GB, (g + 1) * GB):
                                pool.indirect_dma_start(
                                    out=sums[:, h, :], out_offset=None, in_=st,
                                    in_offset=bass.IndirectOffsetOnAxis(ap=last_chunk[:, h:h + 1], axis=0)).then_inc(s_g[g], 16)
                    nsteps(pool, step)

                @block.vector
                def _(dve):
                    K = 2 * (NQ - 1) * NG + 3 * NG
                    dve.memset(sc[1][:], 0.0).then_inc(s_v6, 1)
                    dve.wait_ge(s_v6, 1)

                    def step(s):
                        def make_a(it, b, i):
                            dve.wait_ge(s_rec[b], s * (8 * IT3) + i * 16 + 16)
                            dve.wait_ge(s_tdone, s * IT3 + it + 1)
                            dve.tensor_tensor(am[b][:], rec[b][:, :, 0:K1].unsqueeze(3).broadcast_to([P, J3, K1, CPT]),
                                              mask4[:].unsqueeze(1).unsqueeze(1).broadcast_to([P, J3, K1, CPT]),
                                              ALU.mult).then_inc(s_a, 1)

                        def scan(it, b, i):
                            dve.wait_ge(s_msg, s * IT3 + it + 3)
                            dve.wait_ge(s_scan, s * IT3 + it)
                            dve.wait_ge(s_tr, s * IT3 + it + 1)
                            dve.tensor_tensor_scan(sc[b][:], carry_m[:, bass.ds(it * NT, NT)], pm[:, 0:NT],
                                                   sc[1 - b][:, NT - 1:NT], ALU.mult, ALU.add).then_inc(s_scan, 1)

                        def body(it, b, i):
                            make_a(it + 1, 1 - b, i + b)
                            scan(it, b, i)
                        make_a(0, 0, 0)
                        pairs(dve, IT3 - 1, body)
                        scan(IT3 - 1, 1, IT3 // 2 - 1)
                        dve.wait_ge(s_tr, s * IT3 + IT3 + 2)
                        dve.memset(sc[1][:, NT - 1:NT], 0.0).then_inc(s_v6, 1)
                        dve.wait_ge(s_cr, s * (16 * (NQ - 1)) + 16 * (NQ - 1))
                        ch = Chain(dve, s_v6, s * (K + 1) + 2)
                        dve.wait_ge(s_v6, s * (K + 1) + 2)

                        def aggregate(g):
                            c = slice(g * GB, (g + 1) * GB)
                            dve.wait_ge(s_g[g], s * (16 * GB) + 16 * GB)
                            agg = cat[:, c, 0:D]
                            ch(dve.tensor_tensor(agg, sums[:, c, :], has_edges[:, c].unsqueeze(2).broadcast_to([P, GB, D]), ALU.mult))
                            for q in range(NQ - 1):
                                ch(dve.tensor_tensor(crt[:], cr[:, q, :].unsqueeze(1).broadcast_to([P, GB, D]),
                                                     spans[:, q, c].unsqueeze(2).broadcast_to([P, GB, D]), ALU.mult))
                                add = dve.tensor_tensor(agg, agg, crt[:], ALU.add)
                                if q < NQ - 2:
                                    ch(add)
                                else:
                                    add.then_inc(s_agg, 1)
                                    dve.wait_ge(s_agg, s * NG + g + 1)

                        def update(g):
                            c = slice(g * GB, (g + 1) * GB)
                            h = cat[:, c, D:2 * D]
                            dve.wait_ge(s_sig, s * NG + g + 1)
                            ch(dve.tensor_tensor(tn[:], rz[:, :, 0:D], pg[:, 0:GB, 3 * D:4 * D], ALU.mult))
                            dve.tensor_tensor(tn[:], tn[:], pg[:, 0:GB, 2 * D:3 * D], ALU.add).then_inc(s_pre, 1)
                            dve.wait_ge(s_tanh, s * NG + g + 1)
                            ch(dve.tensor_tensor(tw[:], h, tn[:], ALU.subtract))
                            ch(dve.tensor_tensor(tw[:], tw[:], rz[:, :, D:2 * D], ALU.mult))
                            dve.tensor_tensor(h, tw[:], tn[:], ALU.add).then_inc(s_new, 1)
                            dve.wait_ge(s_new, s * NG + g + 1)
                        aggregate(0)
                        for g in range(NG):
                            if g + 1 < NG:
                                aggregate(g + 1)
                            update(g)
                        assert ch.n == (2 * (NQ - 1)) * NG + 3 * NG == K, (ch.n, K)
                    nsteps(dve, step)

                @block.tensor
                def _(pe):
                    pe.sem_inc(s_tdone, 2)
                    pe.sem_inc(s_msg, 2)
                    pe.sem_inc(s_tr, 2)

                    def step(s):
                        def turn_scan(it, b):
                            pe.wait_ge(s_scan, s * IT3 + it + 1)
                            pe.wait_ge(s_sc, s * IT3 + it)
                            hold(pe)
                            pe.transpose(px[:, 0:P], sc[b][:], ident_f[:]).then_inc(s_tr, 1)

                        def body(it, b, i, first=False):
                            n = s * IT3 + it
                            pe.wait_ge(s_a, n + 1)
                            for g in range(NB):
                                if g == 2 and not first:
                                    turn_scan(it - 1, 1 - b)
                                if g % (NB // 2) == 0:
                                    pe.wait_ge(s_hg[b][g // (NB // 2)], s * (4 * J3 * IT3) + i * (8 * J3) + 8 * J3)
                                pe.wait_ge(s_ts, n * NB + g + 1)
                                hold(pe)
                                for u in range(g * GPB, (g + 1) * GPB):
                                    for q in range(NQ):
                                        k = slice(q * QP, (q + 1) * QP)
                                        at = (u - g * GPB) * K1 * CPT
                                        last = pe.matmul(pt[g % RING][k, at:at + K1 * CPT], hb[b][k, u, :], am[b][k, u, :, :],
                                                         start=True, stop=True, tile_position=(q * QP, q * QP))
                                last.then_inc(s_t, 1)
                            pe.wait_ge(s_t, n * NB + NB)
                            pe.sem_inc(s_tdone, 1)
                            pe.wait_ge(s_ts, n * NB + NB + RING)
                            pe.wait_ge(s_scan, n)
                            for k in range(K1):
                                last = pe.matmul(pm[:, 0:NT], wb[:, k, :], ts[b][:, k, :], start=(k == 0), stop=(k == K1 - 1))
                            last.then_inc(s_msg, 1)
                        body(0, 0, 0, first=True)
                        body(1, 1, 0)
                        with pe.Fori(1, IT3 // 2) as i:
                            body(i * 2, 0, i)
                            body(i * 2 + 1, 1, i)
                        turn_scan(IT3 - 1, 1)
                        for g in range(NG):
                            pe.wait_ge(s_agg, s * NG + g + 1)
                            pe.wait_ge(s_ct, s * NG + g)
                            for h in range(GB):
                                last = pe.transpose(pt[h // 4][0:2 * D + 2, (h % 4) * P:(h % 4 + 1) * P],
                                                    cat[:, g * GB + h, :], ident_f[:])
                            last.then_inc(s_catt, 1)
                            pe.wait_ge(s_ct, s * NG + g + 1)
                            pe.wait_ge(s_pre, s * NG + g)
                            for h in range(GB):
                                last = pe.matmul(pg[:, h, :], ct[:, h, :], wx[:], start=True, stop=True)
                            last.then_inc(s_gate, 1)
                    nsteps(pe, step)

                @block.scalar
                def _(act):
                    act.sem_inc(s_ts, RING)

                    def step(s):
                        def store(it, b, i):
                            n = s * IT3 + it
                            act.wait_ge(s_tr, n + 3)
                            act.wait_ge(s_st[b], s * (8 * IT3) + i * 16)
                            act.copy(sct[b][:], px[:, 0:P]).then_inc(s_sc, 1)
                            act.wait_ge(s_sc, n + 1)
                            act.dma_start(st_rows[bass.ds(it, 1)].rearrange("a c q d -> (a c) q d"),
                                          sct[b][:].rearrange("c (q d) -> c q d", d=D)).then_inc(s_st[b], 16)

                        def body(it, b, i, first=False):
                            n = s * IT3 + it
                            act.wait_ge(s_msg, n + 1)
                            for g in range(NB):
                                if g == 2 and not first:
                                    store(it - 1, 1 - b, i + b - 1)
                                act.wait_ge(s_t, n * NB + g + 1)
                                w = GPB * CPT
                                act.copy(ts[b][:, :, g * w:(g + 1) * w].rearrange("p k (u c) -> p u k c", c=CPT),
                                         pt[g % RING][:, 0:GPB * K1 * CPT].rearrange("p (u k c) -> p u k c", u=GPB, k=K1)
                                         ).then_inc(s_ts, 1)
                        body(0, 0, 0, first=True)
                        body(1, 1, 0)
                        with act.Fori(1, IT3 // 2) as i:
                            body(i * 2, 0, i)
                            body(i * 2 + 1, 1, i)
                        store(IT3 - 1, 1, IT3 // 2 - 1)
                        for g in range(NG):
                            act.wait_ge(s_catt, s * NG + g + 1)
                            act.wait_ge(s_gate, s * NG + g)
                            act.copy(ct[:, 0:4, :], pt[0][0:2 * D + 2, :].rearrange("p (h l) -> p h l", l=P))
                            act.copy(ct[:, 4:GB, :], pt[1][0:2 * D + 2, 0:(GB - 4) * P].rearrange("p (h l) -> p h l", l=P)).then_inc(s_ct, 1)
                            act.wait_ge(s_gate, s * NG + g + 1)
                            act.wait_ge(s_new, s * NG + g)
                            act.activation(rz[:], pg[:, 0:GB, 0:2 * D], ACT.Sigmoid).then_inc(s_sig, 1)
                            act.wait_ge(s_pre, s * NG + g + 1)
                            act.activation(tn[:], tn[:], ACT.Tanh).then_inc(s_tanh, 1)
                    nsteps(act, step)

            s_g7 = sem("g_made")
            s_sv = sem("spans_made")
            s_ini = sem("first_states")
            s_gs = sem("g_scattered")
            s_gl = [sem(f"g_loaded{b}") for b in range(2)]
            s_rl = [sem(f"rec_loaded{b}") for b in range(2)]
            s_gt = sem("g_transposed")
            s_gsc = sem("g_spread")
            s_gtb = sem("g_spread_transposed")
            s_gc = sem("g_spread_copied")
            s_ex = sem("g_expanded")
            s_exr = sem("expanded_read")
            s_mm = sem("messages_made")
            s_ms = [sem(f"messages_scattered{b}") for b in range(2)]
            s_v7 = sem("message_chain")
            gx_rows = gx.rearrange("(q i c) d -> i c q d", q=NQ, c=NT)
            with ExitStack() as c8:
                sb, pb = alloc(c8)
                tmp = sb("ln_tmp2", [P, HG, D])
                deg = sb("deg", [P, HG])
                rec = [sb(f"rec7_{b}", [P, J3, W3]) for b in range(2)]
                gl = [sb(f"gl{b}", [P, P]) for b in range(2)]
                gsp = [sb(f"gsp{b}", [P, NT]) for b in range(2)]
                gc = [sb(f"gc{b}", [P, P]) for b in range(2)]
                sel = sb("chunk_to_rows", [P, J3, P])
                ms = [sb(f"ms{b}", [P, J3, D + 1]) for b in range(2)]
                sv = sb("span_rows", [P, NQ, D])
                ini = sb("first_state", [P, 1])
                own = sb("own_chunk", [P, 1])
                fx = sb("fx", [P, J3])
                ix = [sb(f"ix{b}", [P, J3], I32) for b in range(2)]
                rc = sb("row_chunk", [P, P])
                rci = sb("row_chunk_i", [P, P], I32)
                pgt = pb("pgt", [P, 512])
                pgb = pb("pgb", [P, 512])
                pex = [pb(f"pex{b}", [P, 4, P]) for b in range(4)]
                block = c8.enter_context(nc.Block())
                G = J3 // 4

                @block.sync
                def _(sp):
                    sp.wait_ge(s_gs, 16 * HB)
                    def load(it, b, i):
                        sp.wait_ge(s_gt, it + 1)
                        sp.dma_start(gl[b][:].rearrange("c (q d) -> c q d", d=D),
                                     gx_rows[bass.ds(it, 1)].rearrange("a c q d -> (a c) q d")).then_inc(s_gl[b], 16)
                        sp.wait_ge(s_mm, it + 1)
                        sp.dma_start(rec[b][:], rows3[bass.ds(it, 1)].rearrange("a p w -> (a p) w")).then_inc(s_rl[b], 16)
                    pairs(sp, IT3, load)

                @block.vector
                def _(dve):
                    ch = Chain(dve, s_cv, steps_v[0])
                    gt = sums
                    ch(dve.tensor_tensor(xs[:], xs[:], cat[:, :, D:2 * D], ALU.add))
                    norm_relu(dve, ch, xs[:], gt[:], tmp[:])
                    ch(dve.memset(dis[:], 0.0))
                    ch(dve.memset(deg[:], 1.0))
                    ch(dve.tensor_scalar(deg[:, 0:HB], node_d[:, 0:HB], 1.0, None, ALU.max))
                    ch(dve.tensor_copy(var[:], deg[:]))
                    dve.sem_inc(s_sq, 1)
                    s_ln[0] += 1
                    dve.wait_ge(s_sqd, s_ln[0])
                    ch(dve.reciprocal(deg[:], var[:]))
                    ch(dve.tensor_scalar(dis[:, 0:HB], node_d[:, 0:HB], 0.5, None, ALU.is_gt))
                    ch(dve.tensor_tensor(dis[:], dis[:], deg[:], ALU.mult))
                    ch(dve.tensor_tensor(gt[:], gt[:], dis[:].unsqueeze(2).broadcast_to([P, HG, D]), ALU.mult))
                    dve.sem_inc(s_g7, 1)
                    ch(dve.memset(sv[:], 0.0))
                    for q in range(NQ - 1):
                        ch(dve.tensor_tensor(tmp[:], gt[:], spans[:, q, :].unsqueeze(2).broadcast_to([P, HG, D]), ALU.mult))
                        ch(dve.tensor_reduce(sv[:, q + 1, :], tmp[:].rearrange("p h d -> p d h"), AX.X, ALU.add))
                    dve.sem_inc(s_sv, 1)
                    dve.wait_ge(s_ini, 1)
                    ch(dve.tensor_copy(gsp[1][:, NT - 1:NT], pgt[:, 0:1]))
                    ch(dve.tensor_scalar(rc[:], iota1_f[:], -1.0, None, ALU.add))
                    ch(dve.tensor_copy(rci[:], rc[:]))
                    ch(dve.tensor_scalar(rci[:], rci[:], QP - 1, CH.bit_length() - 1, ALU.bitwise_and, ALU.logical_shift_right))
                    ch(dve.tensor_copy(rc[:], rci[:]))
                    for u in range(J3):
                        ch(dve.tensor_scalar(own[:], part_f[:], -float(u * CPT), None, ALU.add))
                        ch(dve.tensor_scalar(sel[:, u, :], rc[:], own[:, 0:1], None, ALU.is_equal))
                    steps_v[0] += ch.n
                    dve.sem_inc(s_mm, 2)

                    def body(it, b, i):
                        dve.wait_ge(s_gt, it + 3)
                        dve.wait_ge(s_gsc, it)
                        dve.wait_ge(s_gtb, it + 1)
                        dve.tensor_tensor_scan(gsp[b][:], carry_m[:, bass.ds(it * NT, NT)], pgt[:, 0:NT],
                                               gsp[1 - b][:, NT - 1:NT], ALU.mult, ALU.add).then_inc(s_gsc, 1)
                        dve.wait_ge(s_rl[b], i * 16 + 16)
                        dve.wait_ge(s_ms[b], i * (16 * J3))
                        dve.wait_ge(s_mm, it + 2)
                        dve.tensor_scalar(fx[:], rec[b][:, :, W_ONE], -float(BIG), float(BIG), ALU.mult, ALU.add).then_inc(s_v7, 1)
                        dve.tensor_copy(ix[b][:], rec[b][:, :, W_POS_D].bitcast(I32)).then_inc(s_v7, 1)
                        dve.tensor_copy(ms[b][:, :, D], rec[b][:, :, W_LO_D])
                        dve.wait_ge(s_v7, it * 3 + 2)
                        dve.tensor_tensor(ix[b][:], ix[b][:], fx[:], ALU.add).then_inc(s_v7, 1)
                        dve.wait_ge(s_v7, it * 3 + 3)
                        for g in range(G):
                            dve.wait_ge(s_ex, it * G + g + 1)
                            for q in range(NQ):
                                k = slice(q * QP, (q + 1) * QP)
                                last = dve.tensor_tensor(ms[b][k, 4 * g:4 * g + 4, 0:D], pex[g % 4][k, :, q * D:(q + 1) * D],
                                                         rec[b][k, 4 * g:4 * g + 4, W_WEIGHT:W_WEIGHT + 1].broadcast_to([QP, 4, D]), ALU.mult)
                            last.then_inc(s_exr, 1)
                        dve.wait_ge(s_exr, it * G + G + 4)
                        dve.sem_inc(s_mm, 1)
                    pairs(dve, IT3, body)

                @block.scalar
                def _(act):
                    for n in (2, 3):
                        act.wait_ge(s_sq, n)
                        act.sqrt(var[:], var[:]).then_inc(s_sqd, 1)

                    def body(it, b, i):
                        act.wait_ge(s_gtb, it + 3)
                        act.wait_ge(s_ex, it * G)
                        act.copy(gc[b][:], pgb[:, 0:P]).then_inc(s_gc, 1)
                    pairs(act, IT3, body)

                @block.tensor
                def _(pe):
                    pe.wait_ge(s_sv, 1)
                    pe.matmul(pgt[:, 0:1], sv[:].rearrange("p q d -> p (q d)"), ones_f[:, 0:1], start=True, stop=True).then_inc(s_ini, 1)
                    pe.sem_inc(s_gt, 2)
                    pe.sem_inc(s_gtb, 2)
                    pe.sem_inc(s_exr, 4)

                    def body(it, b, i):
                        pe.wait_ge(s_mm, it + 2)
                        pe.wait_ge(s_gl[b], i * 16 + 16)
                        pe.wait_ge(s_gsc, it)
                        pe.transpose(pgt[:, 0:P], gl[b][:], ident_f[:]).then_inc(s_gt, 1)
                        pe.wait_ge(s_gsc, it + 1)
                        pe.wait_ge(s_gc, it)
                        pe.transpose(pgb[:, 0:P], gsp[b][:], ident_f[:]).then_inc(s_gtb, 1)
                        pe.wait_ge(s_gc, it + 1)
                        for g in range(G):
                            pe.wait_ge(s_exr, it * G + g + 1)
                            for u in range(4 * g, 4 * g + 4):
                                last = pe.matmul(pex[g % 4][:, u - 4 * g, :], sel[:, u, :], gc[b][:], start=True, stop=True)
                            last.then_inc(s_ex, 1)
                    pairs(pe, IT3, body)

                @block.gpsimd
                def _(pool):
                    pool.wait_ge(s_g7, 1)
                    for h in range(HB):
                        pool.indirect_dma_start(
                            out=gx, out_offset=bass.IndirectOffsetOnAxis(ap=flag_at[:, h:h + 1], axis=0),
                            in_=sums[:, h, :], in_offset=None, bounds_check=NCH - 1, oob_is_err=False).then_inc(s_gs, 16)

                    def scatter(it, b, i):
                        pool.wait_ge(s_mm, it + 3)
                        hold(pool)
                        for u in range(J3):
                            pool.indirect_dma_start(
                                out=m2, out_offset=bass.IndirectOffsetOnAxis(ap=ix[b][:, u:u + 1], axis=0),
                                in_=ms[b][:, u, :], in_offset=None,
                                bounds_check=T2 * P - 1, oob_is_err=False).then_inc(s_ms[b], 16)
                    pairs(pool, IT3, scatter)
                    for b in range(2):
                        pool.wait_ge(s_ms[b], 16 * J3 * (IT3 // 2))

            s_ldn = [sem(f"messages_loaded{b}") for b in range(2)]
            s_on = sem("onehots_n")
            s_sum = sem("messages_summed")
            s_acc0 = sem("sums_cleared")
            s_z8 = sem("zeros_8")
            s_y = sem("y_made")
            s_out = sem("out_stored")
            rows8 = m2.rearrange("(i p u) w -> i p (u w)", p=P, u=J2)
            with ExitStack() as c9:
                sb, pb = alloc(c9)
                mr = [sb(f"mr{b}", [P, J2, D + 1]) for b in range(2)]
                on = [sb(f"on{b}", [P, J2, P]) for b in range(2)]
                zero = sb("zero8", [P, 512])
                y = sb("y", [P, HB, D])
                acc = pb("node_sums", [P, 7 * 512])
                block = c9.enter_context(nc.Block())
                G = J2 // 4

                @block.sync
                def _(sp):
                    def load(it, b, i):
                        sp.wait_ge(s_sum, it + 1)
                        sp.dma_start(mr[b][:], rows8[bass.ds(it, 1)].rearrange("a p w -> (a p) w")).then_inc(s_ldn[b], 16)
                    pairs(sp, IT2, load)
                    sp.wait_ge(s_y, 1)
                    n = 0
                    if FULL:
                        sp.dma_start(node_rows(out, FULL * P), y[:, 0:FULL, :]).then_inc(s_out, 16)
                        n += 16
                    if REST:
                        sp.dma_start(out[FULL * P:N, :], y[0:REST, FULL, :]).then_inc(s_out, 16)
                        n += 16
                    sp.wait_ge(s_out, n)

                @block.vector
                def _(dve):
                    dve.memset(zero[:], 0.0).then_inc(s_z8, 1)

                    def build(it, b, i):
                        dve.wait_ge(s_ldn[b], i * 16 + 16)
                        dve.wait_ge(s_sum, it + 1)
                        for u in range(J2):
                            last = dve.tensor_scalar(on[b][:, u, :], iota1_f[:], mr[b][:, u, D:D + 1], None, ALU.is_equal)
                        last.then_inc(s_on, 1)
                    pairs(dve, IT2, build)
                    dve.wait_ge(s_sum, IT2 + 2)
                    ch = Chain(dve, s_cv, steps_v[0])
                    ch(dve.tensor_tensor(y[:], acc[:, 0:HB * D].rearrange("p (h d) -> p h d", d=D),
                                         dis[:, 0:HB].unsqueeze(2).broadcast_to([P, HB, D]), ALU.mult))
                    dve.tensor_tensor(y[:], y[:], xs[:, 0:HB, :], ALU.add).then_inc(s_y, 1)

                @block.tensor
                def _(pe):
                    pe.sem_inc(s_sum, 2)
                    pe.wait_ge(s_z8, 1)
                    for k in range(7):
                        pe.matmul(acc[:, 512 * k:512 * k + 512], zero[:, 0:P], zero[:], start=True, stop=False, skip_group_check=True)

                    def body(it, b, i):
                        regs = [hi_registers(pe, pack_d, it * G + g) for g in range(G)]
                        pe.wait_ge(s_on, it + 1)
                        for u in range(J2):
                            last = pe.matmul(acc[:, bass.ds(regs[u // 4][u % 4] * D, D)], on[b][:, u, :], mr[b][:, u, 0:D],
                                             start=False, stop=False, skip_group_check=True)
                        last.then_inc(s_sum, 1)
                    pairs(pe, IT2, body)


_INS = ["x", "src", "dst", "edge_attr_16", "edge_weight", "L0_gnn_W_bond", "L0_gnn_b_bond", "L0_gnn_W_ih",
        "L0_gnn_W_hh", "L0_gnn_b_ih", "L0_gnn_b_hh"]


def kernel(**inputs):
    import numpy as _np
    import concourse.bacc as _bacc
    from concourse import mybir as _mybir
    from concourse.bass_utils import run_bass_kernel_spmd as _run

    nc = _bacc.Bacc("TRN2", target_bir_lowering=False, num_devices=1)
    arrays, args = {}, []
    for name in _INS:
        a = _np.ascontiguousarray(inputs[name])
        arrays[f"in_{name}_dram"] = a
        args.append(nc.dram_tensor(f"in_{name}_dram", a.shape, _mybir.dt.from_np(a.dtype), kind="ExternalInput").ap())
    shape = inputs["x"].shape
    args.append(nc.dram_tensor("out_0_dram", shape, _mybir.dt.float32, kind="ExternalOutput").ap())
    gnn_program(nc, *args)
    r = _run(nc, [arrays], core_ids=[0])
    return r.results[0]["out_0_dram"]
```
